# Optimizing a Trainium2 kernel written in Bass

```python
import numpy as np
import jax
import jax.numpy as jnp

def _softmax(x, axis=-1):
    return jax.nn.softmax(x, axis=axis)

def _gelu(x):
    return jax.nn.gelu(x, approximate=True)

def _silu(x):
    return jax.nn.silu(x)

def _sigmoid(x):
    return jax.nn.sigmoid(x)

def _layernorm(x, axis=-1, eps=1e-05):
    m = jnp.mean(x, axis=axis, keepdims=True)
    v = jnp.var(x, axis=axis, keepdims=True)
    return (x - m) / jnp.sqrt(v + eps)

def _scatter_add(tgt, idx, src, axis=0):
    return tgt.at[idx].add(src)

def _segment_sum(src, seg, n):
    return jax.ops.segment_sum(src, seg, n)
kernel_name = 'mk_adj_resnorm_d4_adj_r2_21c3e9'

def setup_inputs(seed: int=0):
    np.random.seed(seed)
    _w = jnp.asarray

    def _rec_inputs():
        import jax
        import jax.numpy as jnp
        _gk = jax.random.key(seed)
        x = -0.0005207 + 1.001 * jax.random.normal(jax.random.fold_in(_gk, 1), (8192, 128), jnp.float32)
        _w = (1.0 + jnp.arange(8192, dtype=jnp.float32)) ** (-0.5)
        _w = _w / _w.mean()
        _pij = jnp.clip(0.00195312 * _w[:, None] * _w[None, :], 0.0, 1.0)
        _a = jax.random.uniform(jax.random.fold_in(_gk, 2), (8192, 8192)) < _pij
        adj = _a.astype(jnp.int32)
        return (x, adj)
    x, adj = _rec_inputs()

    def _L0_gnn_setup():
        import jax, jax.numpy as jnp
        import numpy as np
        N, D = (4096, 128)
        NEG_BIG = -9000000000000000.0
        key = jax.random.key(seed)
        k1, k2, k3 = jax.random.split(key, 3)
        h = jax.random.normal(k1, (N, D), dtype=jnp.float32)
        adj = jax.random.randint(k2, (N, N), 0, 2, dtype=jnp.int32)
        bound = np.sqrt(6.0 / (2 * D + 1)).astype(np.float32)
        a = jax.random.uniform(k3, (2 * D, 1), dtype=jnp.float32, minval=-bound, maxval=bound)
        return {'h': h, 'adj': adj, 'a': a}
    _L0_gnn_all = _L0_gnn_setup()
    _L0_gnn_in = {k: v for k, v in _L0_gnn_all.items() if k in ('a',)}
    del _L0_gnn_all

    def _L1_gnn_setup():
        import jax, jax.numpy as jnp
        import numpy as np
        N, IN_DIM, OUT_DIM = (4096, 128, 128)
        NEG_INF = -1000000000.0
        key = jax.random.key(seed)
        k1, k2, k3, k4 = jax.random.split(key, 4)
        X = jax.random.normal(k1, (N, IN_DIM), dtype=jnp.float32)
        A = jax.random.randint(k2, (N, N), 0, 2).astype(jnp.int32)
        W_fc = jax.random.normal(k3, (IN_DIM, OUT_DIM), dtype=jnp.float32) * (1.0 / np.sqrt(IN_DIM))
        b_fc = jnp.zeros((OUT_DIM,), dtype=jnp.float32)
        w_att = jax.random.normal(k4, (2 * OUT_DIM,), dtype=jnp.float32) * (1.0 / np.sqrt(2 * OUT_DIM))
        b_att = jnp.zeros((), dtype=jnp.float32)
        return {'X': X, 'A': A, 'W_fc': W_fc, 'b_fc': b_fc, 'w_att': w_att, 'b_att': b_att}
    _L1_gnn_all = _L1_gnn_setup()
    _L1_gnn_in = {k: v for k, v in _L1_gnn_all.items() if k in ('W_fc', 'b_fc', 'w_att', 'b_att')}
    del _L1_gnn_all

    def _L2_gnn_setup():
        import jax, jax.numpy as jnp
        import numpy as np
        N, F_IN, F_OUT = (4096, 128, 128)
        ALPHA = 0.2
        NEG = -9000000000000000.0
        key = jax.random.key(seed)
        k1, k2, k3, k4, k5 = jax.random.split(key, 5)
        h = jax.random.normal(k1, (N, F_IN), dtype=jnp.float32)
        adj = jax.random.randint(k2, (N, N), 0, 2, dtype=jnp.int32)
        W_w = jax.random.normal(k3, (F_IN, F_OUT), dtype=jnp.float32) / np.sqrt(F_IN)
        W_b = jax.random.normal(k4, (F_OUT,), dtype=jnp.float32) * 0.01
        a = jax.random.normal(k5, (2 * F_OUT, 1), dtype=jnp.float32) / np.sqrt(2 * F_OUT)
        return {'h': h, 'adj': adj, 'W_w': W_w, 'W_b': W_b, 'a': a}
    _L2_gnn_all = _L2_gnn_setup()
    _L2_gnn_in = {k: v for k, v in _L2_gnn_all.items() if k in ('W_w', 'W_b', 'a')}
    del _L2_gnn_all

    def _L3_gnn_setup():
        import jax, jax.numpy as jnp
        import numpy as np
        N = 4096
        F_IN = 128
        F_OUT = 128
        ALPHA = 0.2
        NEG_BIG = -9000000000000000.0
        key = jax.random.key(seed)
        k1, k2, k3, k4 = jax.random.split(key, 4)
        h = jax.random.normal(k1, (N, F_IN), dtype=jnp.float32)
        adj = jax.random.randint(k2, (N, N), 0, 2, dtype=jnp.int32)
        W = jax.random.normal(k3, (F_IN, F_OUT), dtype=jnp.float32) * (1.414 / np.sqrt(F_IN))
        a = jax.random.normal(k4, (2 * F_OUT, 1), dtype=jnp.float32) * (1.414 / np.sqrt(2 * F_OUT))
        return {'h': h, 'adj': adj, 'W': W, 'a': a}
    _L3_gnn_all = _L3_gnn_setup()
    _L3_gnn_in = {k: v for k, v in _L3_gnn_all.items() if k in ('W', 'a')}
    del _L3_gnn_all
    return {'x': x, 'adj': adj, 'L0_gnn_a': _L0_gnn_in['a'], 'L1_gnn_W_fc': _L1_gnn_in['W_fc'], 'L1_gnn_b_fc': _L1_gnn_in['b_fc'], 'L1_gnn_w_att': _L1_gnn_in['w_att'], 'L1_gnn_b_att': _L1_gnn_in['b_att'], 'L2_gnn_W_w': _L2_gnn_in['W_w'], 'L2_gnn_W_b': _L2_gnn_in['W_b'], 'L2_gnn_a': _L2_gnn_in['a'], 'L3_gnn_W': _L3_gnn_in['W'], 'L3_gnn_a': _L3_gnn_in['a']}

def reference(x, adj, L0_gnn_a, L1_gnn_W_fc, L1_gnn_b_fc, L1_gnn_w_att, L1_gnn_b_att, L2_gnn_W_w, L2_gnn_W_b, L2_gnn_a, L3_gnn_W, L3_gnn_a):
    import jax
    import jax.numpy as jnp

    def _L0_gnn_ref(h, adj, a):
        import jax, jax.numpy as jnp
        import numpy as np
        N, D = (4096, 128)
        NEG_BIG = -9000000000000000.0
        d = h.shape[1]
        h1 = h @ a[:d]
        h2 = h @ a[d:]
        e = jax.nn.leaky_relu(h1 + h2.T, negative_slope=0.01)
        attention = jnp.where(adj > 0, e, NEG_BIG)
        attention = jax.nn.softmax(attention, axis=1)
        return attention @ h

    def _L1_gnn_ref(X, A, W_fc, b_fc, w_att, b_att):
        import jax, jax.numpy as jnp
        import numpy as np
        N, IN_DIM, OUT_DIM = (4096, 128, 128)
        NEG_INF = -1000000000.0
        H = X @ W_fc + b_fc
        d = H.shape[1]
        s_src = H @ w_att[:d]
        s_dst = H @ w_att[d:]
        scores = s_src[:, None] + s_dst[None, :] + b_att
        scores = jnp.where(A > 0, scores, jnp.float32(NEG_INF))
        alpha = jax.nn.softmax(scores, axis=1)
        return alpha @ H

    def _L2_gnn_ref(h, adj, W_w, W_b, a):
        import jax, jax.numpy as jnp
        import numpy as np
        N, F_IN, F_OUT = (4096, 128, 128)
        ALPHA = 0.2
        NEG = -9000000000000000.0
        Wh = h @ W_w + W_b
        a1 = a[:F_OUT, 0]
        a2 = a[F_OUT:, 0]
        e = jax.nn.leaky_relu((Wh @ a1)[:, None] + (Wh @ a2)[None, :], negative_slope=ALPHA)
        attention = jnp.where(adj > 0, e, NEG)
        attention = jax.nn.softmax(attention, axis=1)
        h_prime = attention @ Wh
        return h_prime

    def _L3_gnn_ref(h, adj, W, a):
        import jax, jax.numpy as jnp
        import numpy as np
        N = 4096
        F_IN = 128
        F_OUT = 128
        ALPHA = 0.2
        NEG_BIG = -9000000000000000.0
        wh = h @ W
        wh1 = wh @ a[:F_OUT, :]
        wh2 = wh @ a[F_OUT:, :]
        e = wh1 + wh2.T
        e = jnp.where(e > 0, e, ALPHA * e)
        e = jnp.where(adj > 0, e, NEG_BIG)
        attention = jax.nn.softmax(e, axis=-1)
        h_prime = attention @ wh
        return jax.nn.elu(h_prime)
    x = _layernorm(x + _L0_gnn_ref(x, adj, L0_gnn_a), axis=-1)
    x = _layernorm(x + _L1_gnn_ref(x, adj, L1_gnn_W_fc, L1_gnn_b_fc, L1_gnn_w_att, L1_gnn_b_att), axis=-1)
    x = _layernorm(x + _L2_gnn_ref(x, adj, L2_gnn_W_w, L2_gnn_W_b, L2_gnn_a), axis=-1)
    x = _layernorm(x + _L3_gnn_ref(x, adj, L3_gnn_W, L3_gnn_a), axis=-1)
    return x

_drawn_inputs = setup_inputs


def setup_inputs(seed=0):
    import zlib

    import numpy as np

    out = dict(_drawn_inputs(seed))
    spreads = {'L1_gnn_b_fc': (0.0, 0.1)}
    factors = {'L2_gnn_W_b': 4.95}
    for name, (base, spread) in spreads.items():
        noise = np.random.default_rng([zlib.crc32(name.encode()), seed]).standard_normal(out[name].shape)
        drawn = base * np.exp(spread * noise) if base else spread * noise
        out[name] = jnp.asarray(drawn.astype(out[name].dtype))
    for name, factor in factors.items():
        out[name] = (out[name] * factor).astype(out[name].dtype)
    return out
```

```python
from contextlib import ExitStack

import concourse.bass as bass
from concourse import mybir

P = 128
D = 128
TILES = 4
W = TILES * P
CHUNKS = 8
PB = 2 * CHUNKS
PCOLS = PB * P
BUFS = 8
LAYERS = 4
SLOPE = [0.01, None, 0.2, 0.2]
EPS = 1e-5
KAPPA = 8.0
CAP = 78.0
VC = D + 1
VR = D + 2

ALU = mybir.AluOpType
ACT = mybir.ActivationFunctionType
AX = mybir.AxisListType
F32 = mybir.dt.float32
F32R = mybir.dt.float32r
BF16 = mybir.dt.bfloat16
U8 = mybir.dt.uint8
U16 = mybir.dt.uint16
I32 = mybir.dt.int32
RMAX = bass.bass_isa.ReduceOp.max


class Chain:

    def __init__(self, engine, semaphore):
        self.engine, self.semaphore, self.at = engine, semaphore, 0

    def then(self, instruction):
        instruction.then_inc(self.semaphore, 1)
        self.at = self.at + 1
        self.engine.wait_ge(self.semaphore, self.at)


def gat4(nc, x, adj, a0, w1, b1, a1, w2, b2, a2, w3, a3, out):
    N = x.shape[0]
    NB = N // P
    S = NB // TILES
    PARTS = NB // PB
    JB = NB * S

    TAIL = [6, 8, 7, 9]

    with ExitStack() as ctx:
        def sb(name, shape, dt, stack=ctx):
            return stack.enter_context(nc.sbuf_tensor(name, shape, dt))

        def sem(name):
            return ctx.enter_context(nc.semaphore(name))

        X = sb("X", [P, NB, D], F32)
        XT = sb("XT", [P, N], F32)
        mask = sb("mask", [P, PARTS, TILES * PCOLS], U8)
        ident = sb("ident", [P, P], F32)
        ident16 = sb("ident16", [P, P], BF16)
        ones = sb("ones", [P, P], F32)
        zeros = sb("zeros", [P, W], BF16)
        Wl = {1: sb("W1", [P, D], F32), 2: sb("W2", [P, D], F32), 3: sb("W3", [P, D], F32)}
        WT = sb("WT", [P, D], F32)
        acol = [sb(f"acol{l}", [P, 2], F32) for l in range(LAYERS)]
        Wa = {0: acol[0], 1: sb("Wa1", [P, 2], F32), 2: sb("Wa2", [P, 2], F32), 3: sb("Wa3", [P, 2], F32)}
        Wsrc = {l: sb(f"Wsrc{l}", [P, P], F32) for l in (0, 2, 3)}
        bias_rows = {1: sb("bias1", [P, D], F32), 2: sb("bias2", [P, D], F32)}
        bcol = sb("bcol", [P, 1], F32)
        bcols = sb("bcols", [P, P], F32)
        bdot = sb("bdot", [P, 2], F32)
        beta = sb("beta", [P, 1], F32)
        tcol = sb("tcol", [P, NB], F32)
        tpart = sb("tpart", [P, 1], F32)
        tmax = sb("tmax", [P, 1], F32)
        sbias = sb("sbias", [P, 1], F32)
        ccol = sb("ccol", [P, NB], F32)
        vcol = sb("vcol", [P, NB], F32)
        xsum = sb("xsum", [P, S], F32)
        xtot = sb("xtot", [P, 1], F32)
        xrows = sb("xrows", [P, P], F32)
        mean = sb("mean", [P, D], F32)
        yraw = sb("yraw", [P, 2, TILES, D], F32)
        flag = sb("flag", [P, TILES], F32)
        den = sb("den", [P, TILES], F32)
        rinv = sb("rinv", [P, TILES], F32)
        G = sb("G", [P, TILES, D], F32)
        Z = sb("Z", [P, TILES, D], F32)
        low = sb("low", [P, TILES, VC], F32)
        stats = sb("stats", [P, TILES, 6], F32)
        mv = sb("mv", [P, TILES, 2], F32)
        spread = sb("spread", [P, TILES], F32)
        minus = sb("minus", [P, TILES], F32)
        power = sb("power", [P, TILES], F32)
        rstd = sb("rstd", [P, TILES], F32)
        shift = sb("shift", [P, TILES], F32)
        Xnew = sb("Xnew", [P, TILES, D], F32)
        XTnew = sb("XTnew", [P, W], F32)

        with ExitStack() as plain:
            pair = sb("pair", [P, BUFS, W], F32, plain)
            y = sb("y", [P, NB, VC], F32, plain)
            adj_in = sb("adj_in", [P, TILES, PCOLS], I32, plain)
            bytes_in = sb("bytes_in", [P, 2, PCOLS], U8, plain)
        pair_r = sb("pair_r", [P, BUFS, W], F32R)
        y_r = sb("y_r", [P, NB, 2, VR], F32R)

        ps = ctx.enter_context(nc.psum_tensor("ps", [P, 8, 512], F32))
        scratch = nc.dram_tensor("mask_scratch", (S, PARTS, P, TILES * PCOLS), U8, kind="Internal").ap()

        x_loaded = sem("x_loaded")
        consts_loaded = sem("consts_loaded")
        adj_loaded = [sem(f"adj_loaded{t}") for t in range(TILES)]
        mask_saved = [sem(f"mask_saved{m}") for m in range(PARTS)]
        mask_loaded = [sem(f"mask_loaded{m}") for m in range(PARTS)]
        ident_zeroed = sem("ident_zeroed")
        ident_made = sem("ident_made")
        fills_made = sem("fills_made")
        w_turned = sem("w_turned")
        w_turn_kept = sem("w_turn_kept")
        wa_summed = sem("wa_summed")
        wa_kept = sem("wa_kept")
        wsrc_made = sem("wsrc_made")
        piece_compared = sem("piece_compared")
        piece_turned = sem("piece_turned")
        piece_kept = sem("piece_kept")
        pair_made = sem("pair_made")
        pair_free = sem("pair_free")
        sums_done = sem("sums_done")
        low_kept = sem("low_kept")
        sums_read = sem("sums_read")
        elu_asked = sem("elu_asked")
        elu_done = sem("elu_done")
        moments_made = sem("moments_made")
        rstd_made = sem("rstd_made")
        norm_ready = sem("norm_ready")
        x_new = sem("x_new")
        x_kept = sem("x_kept")
        x_turned = sem("x_turned")
        xt_new = sem("xt_new")
        xt_kept = sem("xt_kept")
        t_summed = sem("t_summed")
        t_kept = sem("t_kept")
        out_saved = sem("out_saved")
        tpart_made = sem("tpart_made")
        tmax_made = sem("tmax_made")
        exponents_made = sem("exponents_made")
        exps_made = sem("exps_made")
        xrows_made = sem("xrows_made")
        mean_summed = sem("mean_summed")
        mean_kept = sem("mean_kept")
        v_summed = sem("v_summed")
        yraw_made = sem("yraw_made")
        y_made = sem("y_made")
        s_summed = sem("s_summed")
        s_read = sem("s_read")
        w_made = sem("w_made")
        vec_step = sem("vec_step")
        dve_waited = sem("dve_waited")
        sp_waited = sem("sp_waited")

        x_v = x.rearrange("(c p b) d -> p c (b d)", p=P, b=2)
        out_v = out.rearrange("(s h p b) d -> s p h (b d)", h=2, p=P, b=2)
        adj_v = adj.rearrange("(s h p b) (m j) -> s h b m p j", h=2, p=P, b=2, m=PARTS)
        words = mask[:, :, :].bitcast(I32)
        halves = mask[:, :, :].rearrange("p m (t w) -> p m t w", t=TILES).bitcast(U16)
        pairs = mask[:, :, :].rearrange("p m (t c i b) -> p m t c i b", t=TILES, c=CHUNKS, b=2)
        bytes16 = bytes_in[:, :, :].bitcast(BF16)

        def sums(l, slot):
            if l == 1:
                return ps[:, bass.ds(4 * slot, 4), :]
            return ps[:, bass.ds(2 * slot, 2), :].rearrange("p k (t e) -> p (k t) e", t=2)

        def turn_bank(n):
            return 4 + n % 2

        V_BANKS, S_BANKS, MEAN_BANK = (4, 5), (6, 7), 0
        HAS_S = (0, 2, 3)
        s_before = {l: sum(S for k in HAS_S if k < l) for l in range(LAYERS)}
        v_before = {l: sum(S for k in (1, 2, 3) if k < l) for l in range(LAYERS)}

        def slot_of(s):
            return s % 2

        block = ctx.enter_context(nc.Block())

        @block.sync
        def _(sp):
            def load_piece(s, m, t):
                n = (s * PARTS + m) * TILES + t
                if not (isinstance(n, int) and n < TILES):
                    sp.wait_ge(piece_compared, n - (TILES - 1))
                sp.dma_start(adj_in[:, t, :], adj_v[s, t // 2, t % 2, m]).then_inc(adj_loaded[t], 16)

            for t in range(2):
                load_piece(0, 0, t)
            xq = NB // 2 // 4
            for k in range(4):
                sp.dma_start(X[:, 2 * xq * k:2 * xq * (k + 1), :].rearrange("p (c b) d -> p c (b d)", b=2),
                             x_v[:, xq * k:xq * (k + 1), :]).then_inc(x_loaded, 16)
            for t in range(2, TILES):
                load_piece(0, 0, t)

            def superblock(s, last):
                for m in range(PARTS):
                    for t in range(TILES):
                        if m + 1 < PARTS:
                            load_piece(s, m + 1, t)
                        elif not last:
                            load_piece(s + 1, 0, t)
                    sp.wait_ge(piece_kept, TILES * (s * PARTS + m + 1))
                    sp.sem_inc(sp_waited, 1)
                    sp.dma_start(scratch[s, m].bitcast(I32), words[:, m, :])\
                        .then_inc(mask_saved[m], 16)

            with sp.Fori(0, S - 1) as s:
                superblock(s, False)
            superblock(S - 1, True)

            for l in range(1, LAYERS):
                with sp.Fori(0, S) as s:
                    for m in range(PARTS):
                        sp.wait_ge(mask_saved[m], 16 * S)
                        sp.wait_ge(pair_made, ((l * S - 1 + s) * PARTS + m + 1) * PB)
                        sp.sem_inc(sp_waited, 1)
                        sp.dma_start(words[:, m, :], scratch[s, m].bitcast(I32))\
                            .then_inc(mask_loaded[m], 16)

        @block.gpsimd
        def _(pool):
            nc.gpsimd.memset(ident[:, :], 0.0).then_inc(ident_zeroed, 1)
            nc.gpsimd.memset(ident16[:, :], 0.0).then_inc(ident_zeroed, 1)
            nc.gpsimd.memset(power[:, :], -0.5).then_inc(ident_zeroed, 1)
            pool.wait_ge(ident_zeroed, 3)
            for i in (ident, ident16):
                nc.gpsimd.affine_select(out=i[:, :], in_=i[:, :], compare_op=ALU.not_equal, fill=1.0, base=0,
                                        pattern=[[-1, P]], channel_multiplier=1).then_inc(ident_made, 1)

            def keep(l, s):
                pool.wait_ge(moments_made, 2 * (l * S + s + 1))
                nc.gpsimd.tensor_tensor(rstd[:, :], spread[:, :], power[:, :], ALU.pow).then_inc(rstd_made, 1)
                pool.wait_ge(rstd_made, l * S + s + 1)
                nc.gpsimd.tensor_tensor(shift[:, :], minus[:, :], rstd[:, :], ALU.mult).then_inc(norm_ready, 1)
                pool.wait_ge(x_new, l * S + s + 1)
                nc.gpsimd.tensor_copy(X[:, bass.ds(TILES * s, TILES), :], Xnew[:, :, :]).then_inc(x_kept, 1)
                if l == LAYERS - 1:
                    pool.wait_ge(x_kept, l * S + s + 1)
                    nc.gpsimd.dma_start(out_v[s], X[:, bass.ds(TILES * s, TILES), :]
                                        .rearrange("p (h b) d -> p h (b d)", b=2)).then_inc(out_saved, 16)
                    return
                pool.wait_ge(xt_new, S + l * S + s + 1)
                nc.gpsimd.tensor_copy(XT[:, bass.ds(W * s, W)], XTnew[:, :]).then_inc(xt_kept, 1)

            for l in range(LAYERS):
                pool.wait_ge(tpart_made, l + 1)
                nc.gpsimd.partition_all_reduce(tmax[:, :], tpart[:, :], P, RMAX).then_inc(tmax_made, 1)
                with pool.Fori(0, S) as s:
                    keep(l, s)
            pool.wait_ge(out_saved, 16 * S)

        @block.scalar
        def _(act):
            for l, a in enumerate((a0, a1, a2, a3)):
                with nc.allow_non_contiguous_dma(reason="256 numbers"):
                    act.dma_start(acol[l][:, :], a.rearrange("(h k) -> k h", h=2)).then_inc(consts_loaded, 16)
            for l, w in ((1, w1), (2, w2), (3, w3)):
                act.dma_start(Wl[l][:, :], w).then_inc(consts_loaded, 16)
            for l, b in ((1, b1), (2, b2)):
                act.dma_start(bias_rows[l][:, :], b.rearrange("(a d) -> a d", a=1).broadcast_to([P, D]))\
                    .then_inc(consts_loaded, 16)
            with nc.allow_non_contiguous_dma(reason="128 numbers"):
                act.dma_start(bcol[:, :], b2.rearrange("(d a) -> d a", a=1)).then_inc(consts_loaded, 16)

            def keep_piece(s, m, t):
                n = (s * PARTS + m) * TILES + t
                act.wait_ge(piece_turned, n + 1)
                if t == 0 and not (isinstance(s, int) and s == 0):
                    act.wait_ge(pair_made, ((s - 1) * PARTS + m + 1) * PB)
                    act.wait_ge(mask_saved[m], 16 * s)
                nc.scalar.activation(halves[:, m, t, :], ps[:, turn_bank(t), :].bitcast(U16), ACT.Copy)\
                    .then_inc(piece_kept, 1)

            def turned(l, s, where, bank, static):
                act.wait_ge(x_turned, (l + 1) * S + s + 1)
                if not static:
                    if not (isinstance(s, int) and s == 0 and l == 0):
                        act.wait_ge(xt_kept, l * S + s)
                        act.wait_ge(t_summed, (l + 1) * S + s)
                nc.scalar.activation(where, bank, ACT.Copy, accum_out=xsum[:, bass.ds(s, 1)]).then_inc(xt_new, 1)

            def keep_t(l, s, bank):
                act.wait_ge(t_summed, (l + 1) * S + s + 1)
                nc.scalar.activation(tcol[:, bass.ds(TILES * s, TILES)], bank, ACT.Copy).then_inc(t_kept, 1)

            for s in range(S):
                turned(-1, s, XT[:, W * s:W * (s + 1)], ps[:, 4 + s % 2, :], True)
                if s:
                    keep_t(-1, s - 1, ps[:, 6 + (s - 1) % 2, 0:TILES])
            keep_t(-1, S - 1, ps[:, 6 + (S - 1) % 2, 0:TILES])
            for t in range(TILES):
                keep_piece(0, 0, t)

            def between(l):
                act.wait_ge(exponents_made, l + 1)
                if l != 1:
                    nc.scalar.activation(ccol[:, :], ccol[:, :], ACT.Exp)
                nc.scalar.activation(vcol[:, :], vcol[:, :], ACT.Exp).then_inc(exps_made, 1)
                act.wait_ge(mean_summed, l + 1)
                nc.scalar.activation(mean[:, :], ps[:, MEAN_BANK, 0:D], ACT.Copy).then_inc(mean_kept, 1)
                act.wait_ge(exps_made, l + 1)
                if l != 1:
                    nc.scalar.activation(y[:, :, D], vcol[:, :], ACT.Copy).then_inc(y_made, 1)
                if l:
                    for q in range(S):
                        act.wait_ge(v_summed, v_before[l] + q + 1)
                        if l == 1 and q >= 2:
                            act.wait_ge(y_made, 2 + q - 1)
                        for t in range(TILES):
                            to = yraw[:, q % 2, t, :] if l == 1 else y[:, TILES * q + t, 0:D]
                            last = nc.scalar.activation(to, ps[:, V_BANKS[q % 2], t * D:(t + 1) * D], ACT.Identity,
                                                        scale=vcol[:, TILES * q + t:TILES * q + t + 1])
                        last.then_inc(yraw_made, 1)
                if l in HAS_S:
                    for q in range(S):
                        act.wait_ge(s_read, s_before[l] + q + 1)
                        nc.scalar.activation(XT[:, W * q:W * (q + 1)], XT[:, W * q:W * (q + 1)], ACT.Exp,
                                             scale=1.0 - SLOPE[l]).then_inc(w_made, 1)

            def tail_norm(l, s):
                if l == 1:
                    act.wait_ge(sums_done, l * S + s + 1)
                    if not (isinstance(s, int) and s == 0):
                        act.wait_ge(sums_read, l * S + s)
                    nc.scalar.activation(low[:, :, :], sums(l, slot_of(s))[:, :, VR:VR + VC], ACT.Copy)\
                        .then_inc(low_kept, 1)
                if l == LAYERS - 1:
                    act.wait_ge(elu_asked, s + 1)
                    nc.scalar.activation(G[:, :, :], G[:, :, :], ACT.Exp).then_inc(elu_done, 1)
                act.wait_ge(norm_ready, l * S + s + 1)
                if not (isinstance(s, int) and s == 0 and l == 0):
                    act.wait_ge(x_kept, l * S + s)
                    if l < LAYERS - 1:
                        act.wait_ge(x_turned, (l + 1) * S + s)
                for t in range(TILES):
                    last = nc.scalar.activation(Xnew[:, t, :], Z[:, t, :], ACT.Identity,
                                                bias=shift[:, t:t + 1], scale=rstd[:, t:t + 1])
                last.then_inc(x_new, 1)

            def superblock(l, s, first, last):
                for m in range(PARTS):
                    if l == 0 and (m + 1 < PARTS or not last):
                        for t in range(TILES):
                            keep_piece(s if m + 1 < PARTS else s + 1, (m + 1) % PARTS, t)
                    if m == max(PARTS // 2 - 1, 0) and not first:
                        tail_norm(l, s - 1)
                    if m == PARTS - 2 and not first and l < LAYERS - 1:
                        turned(l, s - 1, XTnew[:, :].rearrange("p (t i) -> p t i", t=TILES),
                               sums(l, slot_of(s - 1))[:, :, 0:P], False)
                if not first and l < LAYERS - 1:
                    keep_t(l, s - 1, sums(l, slot_of(s - 1))[:, :, 250])

            for l in range(LAYERS):
                between(l)
                superblock(l, 0, True, False)
                with act.Fori(1, S - 1) as s:
                    superblock(l, s, False, False)
                superblock(l, S - 1, False, True)
                tail_norm(l, S - 1)
                if l < LAYERS - 1:
                    turned(l, S - 1, XTnew[:, :].rearrange("p (t i) -> p t i", t=TILES),
                           sums(l, slot_of(S - 1))[:, :, 0:P], False)
                    keep_t(l, S - 1, sums(l, slot_of(S - 1))[:, :, 250])

        @block.tensor
        def _(pe):
            pe.sem_inc(pair_free, BUFS)
            pe.wait_ge(ident_made, 2)
            pe.wait_ge(consts_loaded, 16 * 10)
            for l in (1, 2, 3):
                if l > 1:
                    pe.wait_ge(w_turn_kept, l - 1)
                pe.transpose(ps[:, 0, 0:P], Wl[l][:, :], ident[:, :]).then_inc(w_turned, 1)
                pe.wait_ge(w_turn_kept, l)
                if l > 1:
                    pe.wait_ge(wa_kept, l - 1)
                pe.matmul(ps[:, 1, 0:2], WT[:, :], acol[l][:, :], start=True, stop=True).then_inc(wa_summed, 1)
            pe.wait_ge(wa_kept, 3)
            pe.wait_ge(fills_made, 4)
            pe.matmul(ps[:, 1, 0:2], bcols[:, :], acol[2][:, :], start=True, stop=True).then_inc(wa_summed, 1)

            def turn_x(l, s, tiles, to):
                for t in range(TILES):
                    last = pe.transpose(to[:, t, 0:P], tiles[:, t, :], ident[:, :])
                last.then_inc(x_turned, 1)

            def sum_t(l, s, xt, to):
                pe.wait_ge(xt_new, (l + 1) * S + s + 1)
                for t in range(TILES):
                    last = pe.matmul(to[:, t:t + 1], xt[:, t * P:(t + 1) * P], Wa[l + 1][:, 1:2],
                                     start=True, stop=True)
                last.then_inc(t_summed, 1)

            pe.wait_ge(x_loaded, 16 * 4)
            for s in range(S + 1):
                if s < S:
                    if s >= 2:
                        pe.wait_ge(xt_new, s - 1)
                    turn_x(-1, s, X[:, TILES * s:TILES * (s + 1), :],
                           ps[:, 4 + s % 2, :].rearrange("p (t i) -> p t i", t=TILES))
                if s:
                    if s >= 3:
                        pe.wait_ge(t_kept, s - 2)
                    sum_t(-1, s - 1, XT[:, W * (s - 1):W * s], ps[:, 6 + (s - 1) % 2, :])

            def turn_piece(s, m, t):
                n = (s * PARTS + m) * TILES + t
                pe.wait_ge(piece_compared, n + 1)
                if not (isinstance(n, int) and n < 2):
                    pe.wait_ge(piece_kept, n - 1)
                for c in range(CHUNKS):
                    last = pe.transpose(ps[:, turn_bank(t), :].bitcast(BF16)[:, c * P:(c + 1) * P],
                                        bytes16[:, t % 2, c * P:(c + 1) * P], ident16[:, :])
                last.then_inc(piece_turned, 1)

            pe.wait_ge(xt_new, S)
            for t in range(TILES):
                turn_piece(0, 0, t)

            def between(l):
                pe.wait_ge(xrows_made, l + 1)
                pe.matmul(ps[:, MEAN_BANK, 0:D], xrows[:, :], Wl[l][:, :] if l else ident[:, :],
                          start=True, stop=True).then_inc(mean_summed, 1)
                if l:
                    for q in range(S):
                        pe.wait_ge(xt_kept, l * S)
                        if q >= 2:
                            pe.wait_ge(yraw_made, v_before[l] + q - 1)
                        for t in range(TILES):
                            k = TILES * q + t
                            last = pe.matmul(ps[:, V_BANKS[q % 2], t * D:(t + 1) * D], XT[:, k * P:(k + 1) * P],
                                             Wl[l][:, :], start=True, stop=True)
                        last.then_inc(v_summed, 1)
                if l in HAS_S:
                    pe.wait_ge(wsrc_made, 3)
                    for q in range(S):
                        if q >= 2:
                            pe.wait_ge(s_read, s_before[l] + q - 1)
                        pe.matmul(ps[:, S_BANKS[q % 2], :], Wsrc[l][:, :], XT[:, W * q:W * (q + 1)],
                                  start=True, stop=True).then_inc(s_summed, 1)
                pe.wait_ge(y_made, [2, 2 + S, 3 + S, 4 + S][l])
                if l:
                    pe.wait_ge(yraw_made, v_before[l] + S)
                pe.wait_ge(mean_kept, l + 1)

            def step(l, s, slot, j, buf):
                pe.wait_ge(pair_made, l * JB + s * NB + j + 1)
                to = sums(l, slot)
                for t in range(TILES):
                    if l == 1:
                        last = pe.matmul(to[:, t, 0:2 * VR], pair_r[:, buf, t * P:(t + 1) * P],
                                         y_r[:, bass.ds(j, 1), :, :].rearrange("p a r e -> p (a r e)"),
                                         start=False, stop=False, skip_group_check=True)
                    else:
                        last = pe.matmul(to[:, t, 0:VC], pair[:, buf, t * P:(t + 1) * P],
                                         y[:, bass.ds(j, 1), :].rearrange("p a e -> p (a e)"),
                                         start=False, stop=False, skip_group_check=True)
                last.then_inc(pair_free, 1)
                return last

            def superblock(l, s, slot, first, last):
                if not (isinstance(s, int) and s < 2):
                    if l < LAYERS - 1:
                        pe.wait_ge(t_kept, (l + 1) * S + s - 1)
                    else:
                        pe.wait_ge(sums_read, l * S + s - 1)
                banks = 4 if l == 1 else 2
                for k in range(banks):
                    pe.matmul(ps[:, banks * slot + k, :],
                              zeros[:, 0:P], zeros[:, 0:512],
                              start=True, stop=False, skip_group_check=True)
                for m in range(PARTS):
                    if m == PARTS - 1 and not first and l < LAYERS - 1:
                        pe.wait_ge(x_new, l * S + s)
                        pe.wait_ge(sums_read, l * S + s)
                        turn_x(l, s - 1, Xnew[:, :, :], sums(l, 1 - slot))
                    if l == 0:
                        for j in range(PB):
                            step(l, s, slot, PB * m + j, j % BUFS)
                            if j % TILES == TILES - 1 and (m + 1 < PARTS or not last):
                                turn_piece(s if m + 1 < PARTS else s + 1, (m + 1) % PARTS, j // TILES)
                    else:
                        with pe.Fori(0, PB // BUFS) as h:
                            for j in range(BUFS):
                                step(l, s, slot, PB * m + h * BUFS + j, j)
                done(l, slot)
                if not first and l < LAYERS - 1:
                    sum_t(l, s - 1, XTnew, sums(l, 1 - slot)[:, :, 250])

            def done(l, slot):
                pe.matmul(sums(l, slot)[:, 0, 0:64], zeros[:, 0:P], zeros[:, 0:64],
                          start=False, stop=True, skip_group_check=True).then_inc(sums_done, 1)

            for l in range(LAYERS):
                between(l)
                superblock(l, 0, 0, True, False)
                with pe.Fori(1, S - 1, 2) as s:
                    superblock(l, s, 1, False, False)
                    superblock(l, s + 1, 0, False, False)
                superblock(l, S - 1, 1, False, True)
                if l < LAYERS - 1:
                    pe.wait_ge(x_new, (l + 1) * S)
                    pe.wait_ge(sums_read, (l + 1) * S)
                    turn_x(l, S - 1, Xnew[:, :, :], sums(l, 1))
                    sum_t(l, S - 1, XTnew, sums(l, 1)[:, :, 250])

        @block.vector
        def _(dve):
            chain = Chain(dve, vec_step)
            nc.vector.memset(ones[:, :], 1.0).then_inc(fills_made, 1)
            nc.vector.memset(zeros[:, :], 0.0).then_inc(fills_made, 1)

            def compare_piece(s, m, t):
                n = (s * PARTS + m) * TILES + t
                dve.wait_ge(adj_loaded[t], 16 * (s * PARTS + m + 1))
                if not (isinstance(n, int) and n < 2):
                    dve.wait_ge(piece_turned, n - 1)
                nc.vector.tensor_scalar(bytes_in[:, t % 2, :], adj_in[:, t, :], 0.0, None, ALU.is_gt)\
                    .then_inc(piece_compared, 1)

            dve.wait_ge(consts_loaded, 16 * 10)
            dve.wait_ge(fills_made, 2)
            nc.vector.tensor_scalar(bcols[:, :], ones[:, :], bcol[:, 0:1], None, ALU.mult).then_inc(fills_made, 1)
            nc.vector.memset(beta[:, :], 0.0).then_inc(fills_made, 1)
            for t in range(2):
                compare_piece(0, 0, t)
            for l in (1, 2, 3):
                dve.wait_ge(w_turned, l)
                if l > 1:
                    dve.wait_ge(wa_summed, l - 1)
                nc.vector.tensor_copy(WT[:, :], ps[:, 0, 0:P]).then_inc(w_turn_kept, 1)
                dve.wait_ge(wa_summed, l)
                nc.vector.tensor_copy(Wa[l][:, :], ps[:, 1, 0:2]).then_inc(wa_kept, 1)
            dve.wait_ge(wa_kept, 3)
            for l in HAS_S:
                nc.vector.tensor_scalar(Wsrc[l][:, :], ones[:, :], Wa[l][:, 0:1], None, ALU.mult)\
                    .then_inc(wsrc_made, 1)
            dve.wait_ge(wa_summed, 4)
            dve.wait_ge(fills_made, 4)
            chain.then(nc.vector.tensor_copy(bdot[:, :], ps[:, 1, 0:2]))
            chain.then(nc.vector.tensor_tensor(beta[:, :], bdot[:, 0:1], bdot[:, 1:2], ALU.add))
            for t in range(2, TILES):
                compare_piece(0, 0, t)

            def between(l):
                dve.wait_ge(t_kept, (l + 1) * S)
                nc.vector.tensor_reduce(tpart[:, :], tcol[:, :], AX.X, ALU.max).then_inc(tpart_made, 1)
                dve.wait_ge(xt_new, (l + 1) * S)
                chain.then(nc.vector.tensor_reduce(xtot[:, :], xsum[:, :], AX.X, ALU.add))
                if l:
                    dve.wait_ge(mean_summed, l)
                nc.vector.tensor_scalar(xrows[:, :], ones[:, :], xtot[:, 0:1], 1.0 / N, ALU.mult, ALU.mult)\
                    .then_inc(xrows_made, 1)
                dve.wait_ge(tmax_made, l + 1)
                chain.then(nc.vector.tensor_scalar(tcol[:, :], tcol[:, :], tmax[:, 0:1], None, ALU.subtract))
                if l != 1:
                    chain.then(nc.vector.tensor_scalar(ccol[:, :], tcol[:, :], -(1.0 - SLOPE[l]), CAP,
                                                       ALU.mult, ALU.min))
                    if l == 2:
                        chain.then(nc.vector.tensor_tensor(sbias[:, :], tmax[:, :], beta[:, :], ALU.add))
                nc.vector.tensor_scalar(vcol[:, :], tcol[:, :], KAPPA, None, ALU.subtract)\
                    .then_inc(exponents_made, 1)
                dve.wait_ge(exps_made, l + 1)
                if l == 0:
                    nc.vector.tensor_tensor(y[:, :, 0:D], X[:, :, :],
                                            vcol[:, :].rearrange("p (q a) -> p q a", a=1).broadcast_to([P, NB, D]),
                                            ALU.mult).then_inc(y_made, 1)
                if l == 1:
                    y32 = y_r[:, :, :, :].bitcast(F32)
                    v3 = vcol[:, :].rearrange("p (q a) -> p q a", a=1)
                    chain.then(nc.vector.tensor_copy(y_r[:, :, 0, D:D + 1], v3))
                    nc.vector.tensor_tensor(y_r[:, :, 1, D:D + 1], v3, y32[:, :, 0, D:D + 1], ALU.subtract)
                    for r in range(2):
                        chain.then(nc.vector.tensor_scalar(y_r[:, :, r, D + 1:D + 2], v3, 0.0, None, ALU.mult))
                    for q in range(S):
                        dve.wait_ge(yraw_made, v_before[l] + q + 1)
                        b = slice(TILES * q, TILES * (q + 1))
                        chain.then(nc.vector.tensor_copy(y_r[:, b, 0, 0:D], yraw[:, q % 2, :, :]))
                        nc.vector.tensor_tensor(y_r[:, b, 1, 0:D], yraw[:, q % 2, :, :], y32[:, b, 0, 0:D],
                                                ALU.subtract).then_inc(y_made, 1)
                if l in HAS_S:
                    guard = sbias if l == 2 else tmax
                    for q in range(S):
                        dve.wait_ge(s_summed, s_before[l] + q + 1)
                        nc.vector.tensor_scalar(XT[:, W * q:W * (q + 1)], ps[:, S_BANKS[q % 2], :], guard[:, 0:1],
                                                CAP / (1.0 - SLOPE[l]), ALU.add, ALU.min).then_inc(s_read, 1)
                    dve.wait_ge(w_made, s_before[l] + S)
                dve.wait_ge(mean_kept, l + 1)

            def step(l, s, m, j, buf):
                dve.wait_ge(pair_free, l * JB + s * NB + PB * m + j + 1)
                bits = pairs[:, m, :, bass.ds(j // 2, 1), :, buf % 2].rearrange("p t c i -> p t (c i)")
                if l == 1:
                    nc.vector.tensor_copy(pair_r[:, buf, :].rearrange("p (t i) -> p t i", t=TILES), bits)\
                        .then_inc(pair_made, 1)
                    return
                nc.vector.scalar_tensor_tensor(pair[:, buf, :].rearrange("p (t i) -> p t i", t=TILES),
                                               XT[:, bass.ds(s * W, W)].rearrange("p (t i) -> p t i", t=TILES),
                                               ccol[:, bass.ds(PB * m + j, 1)], bits,
                                               ALU.max, ALU.mult).then_inc(pair_made, 1)

            def tail(l, s, base):
                chain.at = base
                old = X[:, bass.ds(TILES * s, TILES), :]
                got = sums(l, slot_of(s))
                dve.wait_ge(sums_done, l * S + s + 1)
                if l == 1:
                    dve.wait_ge(low_kept, s + 1)
                    chain.then(nc.vector.tensor_tensor(low[:, :, :], got[:, :, 0:VC], low[:, :, :], ALU.add))
                    got = low
                chain.then(nc.vector.tensor_scalar(flag[:, :], got[:, :, D], 0.0, None, ALU.is_equal))
                chain.then(nc.vector.tensor_tensor(den[:, :], got[:, :, D], flag[:, :], ALU.add))
                chain.then(nc.vector.reciprocal(rinv[:, :], den[:, :]))
                if not (isinstance(s, int) and s == 0 and l == 0):
                    dve.wait_ge(x_new, l * S + s)
                for t in range(TILES):
                    if l < LAYERS - 1:
                        g = nc.vector.scalar_tensor_tensor(G[:, t, :], mean[:, :], flag[:, t:t + 1],
                                                           X[:, bass.ds(TILES * s + t, 1), :].rearrange("p a d -> p (a d)"),
                                                           ALU.mult, ALU.add)
                    else:
                        g = nc.vector.tensor_scalar(G[:, t, :], mean[:, :], flag[:, t:t + 1], None, ALU.mult)
                chain.then(g)
                for t in range(TILES):
                    z = nc.vector.scalar_tensor_tensor(Z[:, t, :], got[:, t, 0:D], rinv[:, t:t + 1], G[:, t, :],
                                                       ALU.mult, ALU.add)
                z.then_inc(sums_read, 1)
                dve.wait_ge(sums_read, l * S + s + 1)
                if l in bias_rows:
                    chain.then(nc.vector.tensor_tensor(
                        Z[:, :, :], Z[:, :, :],
                        bias_rows[l][:, :].rearrange("p (a d) -> p a d", a=1).broadcast_to([P, TILES, D]), ALU.add))
                if l == LAYERS - 1:
                    nc.vector.tensor_scalar(G[:, :, :], Z[:, :, :], 0.0, None, ALU.min).then_inc(elu_asked, 1)
                    chain.then(nc.vector.tensor_scalar(Z[:, :, :], Z[:, :, :], 0.0, None, ALU.max))
                    dve.wait_ge(elu_done, s + 1)
                    chain.then(nc.vector.scalar_tensor_tensor(Z[:, :, :], G[:, :, :], -1.0, Z[:, :, :],
                                                              ALU.add, ALU.add))
                    chain.then(nc.vector.tensor_tensor(Z[:, :, :], Z[:, :, :], old, ALU.add))
                for t in range(TILES):
                    b = nc.vector.bn_stats(stats[:, t, :], Z[:, t, :])
                chain.then(b)
                dve.sem_inc(dve_waited, 1)
                for t in range(TILES):
                    b = nc.vector.bn_aggr(mv[:, t, :], stats[:, t, :])
                chain.then(b)
                nc.vector.tensor_scalar(spread[:, :], mv[:, :, 1], EPS, None, ALU.add).then_inc(moments_made, 1)
                nc.vector.tensor_scalar(minus[:, :], mv[:, :, 0], -1.0, None, ALU.mult).then_inc(moments_made, 1)

            def superblock(l, s, first, last, base):
                for m in range(PARTS):
                    if l == 0:
                        dve.wait_ge(piece_kept, TILES * (s * PARTS + m + 1))
                        for j in range(PB):
                            step(l, s, m, j, j % BUFS)
                            if j % TILES == 0 and (m + 1 < PARTS or not last):
                                compare_piece(s if m + 1 < PARTS else s + 1, (m + 1) % PARTS, j // TILES)
                    else:
                        with dve.Fori(0, PB // BUFS) as h:
                            dve.wait_ge(mask_loaded[m], 16 * ((l - 1) * S + s + 1))
                            for j in range(BUFS):
                                step(l, s, m, h * BUFS + j, j)
                    if m == max(PARTS // 2 - 1, 0) and not first:
                        tail(l, s - 1, base + (s - 1) * TAIL[l])

            for l in range(LAYERS):
                between(l)
                base = chain.at
                superblock(l, 0, True, False, base)
                with dve.Fori(1, S - 1) as s:
                    superblock(l, s, False, False, base)
                superblock(l, S - 1, False, True, base)
                at = base + (S - 1) * TAIL[l]
                assert chain.at == at, (l, base, chain.at, at)
                tail(l, S - 1, at)


_INS = ["x", "adj", "L0_gnn_a", "L1_gnn_W_fc", "L1_gnn_b_fc", "L1_gnn_w_att", "L2_gnn_W_w", "L2_gnn_W_b",
        "L2_gnn_a", "L3_gnn_W", "L3_gnn_a"]


def kernel(**inputs):
    import numpy as _np
    import concourse.bacc as _bacc
    from concourse import mybir as _mybir
    from concourse.bass_utils import run_bass_kernel_spmd as _run

    nc = _bacc.Bacc("TRN2", target_bir_lowering=False, num_devices=1)
    arrays, args = {}, []
    for name in _INS:
        a = _np.ascontiguousarray(inputs[name])
        if name.endswith("_a"):
            a = a.reshape(-1)
        arrays[f"in_{name}_dram"] = a
        args.append(nc.dram_tensor(f"in_{name}_dram", a.shape, _mybir.dt.from_np(a.dtype), kind="ExternalInput").ap())
    n, d = inputs["x"].shape
    args.append(nc.dram_tensor("out_0_dram", (n, d), _mybir.dt.float32, kind="ExternalOutput").ap())
    gat4(nc, *args)
    r = _run(nc, [arrays], core_ids=[0])
    return r.results[0]["out_0_dram"]
```

```python
from contextlib import ExitStack

import concourse.bass as bass
from concourse import mybir

P = 128
D = 128
TILES = 4
W = TILES * P
CHUNKS = 8
PB = 2 * CHUNKS
PCOLS = PB * P
RING = 4
LAYERS = 4
SLOPE = [0.01, None, 0.2, 0.2]
EPS = 1e-5
KAPPA = 8.0
CAP = 78.0
VC = D + 1
VR = D + 2

ALU = mybir.AluOpType
ACT = mybir.ActivationFunctionType
AX = mybir.AxisListType
F32 = mybir.dt.float32
F32R = mybir.dt.float32r
BF16 = mybir.dt.bfloat16
U8 = mybir.dt.uint8
U16 = mybir.dt.uint16
I32 = mybir.dt.int32
RMAX = bass.bass_isa.ReduceOp.max


class Chain:

    def __init__(self, engine, semaphore):
        self.engine, self.semaphore, self.at = engine, semaphore, 0

    def then(self, instruction):
        instruction.then_inc(self.semaphore, 1)
        self.at = self.at + 1
        self.engine.wait_ge(self.semaphore, self.at)


def gat4(nc, x, adj, a0, w1, b1, a1, w2, b2, a2, w3, a3, out):
    N = x.shape[0]
    NB = N // P
    S = NB // TILES
    PARTS = NB // PB
    NC = NB // 2

    TAIL = [6, 8, 7, 9]

    with ExitStack() as ctx:
        def sb(name, shape, dt, stack=ctx):
            return stack.enter_context(nc.sbuf_tensor(name, shape, dt))

        def sem(name):
            return ctx.enter_context(nc.semaphore(name))

        X = sb("X", [P, NB, D], F32)
        XT = sb("XT", [P, N], F32)
        mask = sb("mask", [P, PARTS, TILES * PCOLS], U8)
        ident = sb("ident", [P, P], F32)
        ident16 = sb("ident16", [P, P], BF16)
        ones = sb("ones", [P, P], F32)
        zeros = sb("zeros", [P, W], BF16)
        Wl = {1: sb("W1", [P, D], F32), 2: sb("W2", [P, D], F32), 3: sb("W3", [P, D], F32)}
        WT = sb("WT", [P, D], F32)
        acol = [sb(f"acol{l}", [P, 2], F32) for l in range(LAYERS)]
        Wa = {0: acol[0], 1: sb("Wa1", [P, 2], F32), 2: sb("Wa2", [P, 2], F32), 3: sb("Wa3", [P, 2], F32)}
        Wsrc = {l: sb(f"Wsrc{l}", [P, P], F32) for l in (0, 2, 3)}
        bias_rows = {1: sb("bias1", [P, D], F32), 2: sb("bias2", [P, D], F32)}
        bcol = sb("bcol", [P, 1], F32)
        bcols = sb("bcols", [P, P], F32)
        bdot = sb("bdot", [P, 2], F32)
        beta = sb("beta", [P, 1], F32)
        tcol = sb("tcol", [P, NB], F32)
        tpart = sb("tpart", [P, 1], F32)
        tmax = sb("tmax", [P, 1], F32)
        sbias = sb("sbias", [P, 1], F32)
        ccol = sb("ccol", [P, NB], F32)
        vcol = sb("vcol", [P, NB], F32)
        xsum = sb("xsum", [P, S], F32)
        xtot = sb("xtot", [P, 1], F32)
        xrows = sb("xrows", [P, P], F32)
        mean = sb("mean", [P, D], F32)
        flag = sb("flag", [P, TILES], F32)
        den = sb("den", [P, TILES], F32)
        rinv = sb("rinv", [P, TILES], F32)
        G = sb("G", [P, TILES, D], F32)
        Z = sb("Z", [P, TILES, D], F32)
        stats = sb("stats", [P, TILES, 6], F32)
        mv = sb("mv", [P, TILES, 2], F32)
        spread = sb("spread", [P, TILES], F32)
        minus = sb("minus", [P, TILES], F32)
        power = sb("power", [P, TILES], F32)
        rstd = sb("rstd", [P, TILES], F32)
        shift = sb("shift", [P, TILES], F32)
        Xnew = sb("Xnew", [P, TILES, D], F32)
        XTnew = sb("XTnew", [P, W], F32)

        with ExitStack() as plain:
            pair = sb("pair", [P, RING, 2, W], F32, plain)
            y = sb("y", [P, NB, VC], F32, plain)
            adj_in = sb("adj_in", [P, TILES, PCOLS], I32, plain)
            bytes_in = sb("bytes_in", [P, TILES, PCOLS], U8, plain)
        pair_r = sb("pair_r", [P, RING, 2, W], F32R)
        y_r = sb("y_r", [P, NB, 2, VR], F32R)
        yraw = sb("yraw", [P, 2, TILES, D], F32)
        low = sb("low", [P, TILES, VC], F32)

        ps = ctx.enter_context(nc.psum_tensor("ps", [P, 8, 512], F32))
        scratch = nc.dram_tensor("mask_scratch", (S, PARTS, P, TILES * PCOLS), U8, kind="Internal").ap()

        x_loaded = sem("x_loaded")
        consts_loaded = sem("consts_loaded")
        adj_loaded = [sem(f"adj_loaded{t}") for t in range(TILES)]
        mask_saved = [sem(f"mask_saved{m}") for m in range(PARTS)]
        mask_loaded = [sem(f"mask_loaded{m}") for m in range(PARTS)]
        ident_zeroed = sem("ident_zeroed")
        ident_made = sem("ident_made")
        fills_made = sem("fills_made")
        w_turned = sem("w_turned")
        w_turn_kept = sem("w_turn_kept")
        wa_summed = sem("wa_summed")
        wa_kept = sem("wa_kept")
        wsrc_made = sem("wsrc_made")
        piece_compared = sem("piece_compared")
        piece_turned = sem("piece_turned")
        piece_kept = sem("piece_kept")
        pair_made = sem("pair_made")
        pair_free = sem("pair_free")
        low_kept = sem("low_kept")
        sums_read = sem("sums_read")
        elu_asked = sem("elu_asked")
        elu_done = sem("elu_done")
        moments_made = sem("moments_made")
        rstd_made = sem("rstd_made")
        norm_ready = sem("norm_ready")
        x_new = sem("x_new")
        x_kept = sem("x_kept")
        x_turned = sem("x_turned")
        xt_new = sem("xt_new")
        xt_kept = sem("xt_kept")
        t_summed = sem("t_summed")
        t_kept = sem("t_kept")
        out_saved = sem("out_saved")
        tpart_made = sem("tpart_made")
        tmax_made = sem("tmax_made")
        exponents_made = sem("exponents_made")
        exps_made = sem("exps_made")
        xrows_made = sem("xrows_made")
        mean_summed = sem("mean_summed")
        mean_kept = sem("mean_kept")
        v_summed = sem("v_summed")
        yraw_made = sem("yraw_made")
        y_made = sem("y_made")
        s_summed = sem("s_summed")
        s_read = sem("s_read")
        w_made = sem("w_made")
        vec_step = sem("vec_step")
        dve_waited = sem("dve_waited")
        sp_waited = sem("sp_waited")

        x_v = x.rearrange("(c p b) d -> p c (b d)", p=P, b=2)
        out_v = out.rearrange("(s h p b) d -> s p h (b d)", h=2, p=P, b=2)
        adj_v = adj.rearrange("(s h p b) (m j) -> s h b m p j", h=2, p=P, b=2, m=PARTS)
        words = mask[:, :, :].bitcast(I32)
        halves = mask[:, :, :].rearrange("p m (t w) -> p m t w", t=TILES).bitcast(U16)
        pairs = mask[:, :, :].rearrange("p m (t c i b) -> p m t c i b", t=TILES, c=CHUNKS, b=2)
        bytes16 = bytes_in[:, :, :].bitcast(BF16)

        def sums(l, slot):
            if l == 1:
                return ps[:, bass.ds(4 * slot, 4), :]
            return ps[:, bass.ds(2 * slot, 2), :].rearrange("p k (t e) -> p (k t) e", t=2)

        V_BANKS, S_BANKS, MEAN_BANK = (4, 5), (6, 7), 0
        HAS_S = (0, 2, 3)
        s_before = {l: sum(S for k in HAS_S if k < l) for l in range(LAYERS)}
        v_before = {l: sum(S for k in (1, 2, 3) if k < l) for l in range(LAYERS)}

        def slot_of(s):
            return s % 2

        block = ctx.enter_context(nc.Block())

        @block.sync
        def _(sp):
            def load_piece(s, m, t):
                n = (s * PARTS + m) * TILES + t
                if not (isinstance(n, int) and n < TILES):
                    sp.wait_ge(piece_compared, n - (TILES - 1))
                sp.dma_start(adj_in[:, t, :], adj_v[s, t // 2, t % 2, m]).then_inc(adj_loaded[t], 16)

            for t in range(2):
                load_piece(0, 0, t)
            xq = NB // 2 // 4
            for k in range(4):
                sp.dma_start(X[:, 2 * xq * k:2 * xq * (k + 1), :].rearrange("p (c b) d -> p c (b d)", b=2),
                             x_v[:, xq * k:xq * (k + 1), :]).then_inc(x_loaded, 16)
            for t in range(2, TILES):
                load_piece(0, 0, t)

            def superblock(s, last):
                for m in range(PARTS):
                    for t in range(TILES):
                        if m + 1 < PARTS:
                            load_piece(s, m + 1, t)
                        elif not last:
                            load_piece(s + 1, 0, t)
                    sp.wait_ge(piece_kept, TILES * (s * PARTS + m + 1))
                    sp.sem_inc(sp_waited, 1)
                    sp.dma_start(scratch[s, m].bitcast(I32), words[:, m, :])\
                        .then_inc(mask_saved[m], 16)

            with sp.Fori(0, S - 1) as s:
                superblock(s, False)
            superblock(S - 1, True)

            for l in range(1, LAYERS):
                with sp.Fori(0, S) as s:
                    for m in range(PARTS):
                        sp.wait_ge(mask_saved[m], 16 * S)
                        sp.wait_ge(pair_made, ((l * S - 1 + s) * PARTS + m + 1) * CHUNKS)
                        sp.sem_inc(sp_waited, 1)
                        sp.dma_start(words[:, m, :], scratch[s, m].bitcast(I32))\
                            .then_inc(mask_loaded[m], 16)

        @block.gpsimd
        def _(pool):
            nc.gpsimd.memset(ident[:, :], 0.0).then_inc(ident_zeroed, 1)
            nc.gpsimd.memset(ident16[:, :], 0.0).then_inc(ident_zeroed, 1)
            nc.gpsimd.memset(power[:, :], -0.5).then_inc(ident_zeroed, 1)
            pool.wait_ge(ident_zeroed, 3)
            for i in (ident, ident16):
                nc.gpsimd.affine_select(out=i[:, :], in_=i[:, :], compare_op=ALU.not_equal, fill=1.0, base=0,
                                        pattern=[[-1, P]], channel_multiplier=1).then_inc(ident_made, 1)

            def keep(l, s):
                pool.wait_ge(moments_made, 2 * (l * S + s + 1))
                nc.gpsimd.tensor_tensor(rstd[:, :], spread[:, :], power[:, :], ALU.pow).then_inc(rstd_made, 1)
                pool.wait_ge(rstd_made, l * S + s + 1)
                nc.gpsimd.tensor_tensor(shift[:, :], minus[:, :], rstd[:, :], ALU.mult).then_inc(norm_ready, 1)
                pool.wait_ge(x_new, l * S + s + 1)
                nc.gpsimd.tensor_copy(X[:, bass.ds(TILES * s, TILES), :], Xnew[:, :, :]).then_inc(x_kept, 1)
                if l == LAYERS - 1:
                    pool.wait_ge(x_kept, l * S + s + 1)
                    nc.gpsimd.dma_start(out_v[s], X[:, bass.ds(TILES * s, TILES), :]
                                        .rearrange("p (h b) d -> p h (b d)", b=2)).then_inc(out_saved, 16)
                    return
                pool.wait_ge(xt_new, S + l * S + s + 1)
                nc.gpsimd.tensor_copy(XT[:, bass.ds(W * s, W)], XTnew[:, :]).then_inc(xt_kept, 1)

            for l in range(LAYERS):
                pool.wait_ge(tpart_made, l + 1)
                nc.gpsimd.partition_all_reduce(tmax[:, :], tpart[:, :], P, RMAX).then_inc(tmax_made, 1)
                with pool.Fori(0, S) as s:
                    keep(l, s)
            pool.wait_ge(out_saved, 16 * S)

        @block.scalar
        def _(act):
            for l, a in enumerate((a0, a1, a2, a3)):
                with nc.allow_non_contiguous_dma(reason="256 numbers"):
                    act.dma_start(acol[l][:, :], a.rearrange("(h k) -> k h", h=2)).then_inc(consts_loaded, 16)
            for l, w in ((1, w1), (2, w2), (3, w3)):
                act.dma_start(Wl[l][:, :], w).then_inc(consts_loaded, 16)
            for l, b in ((1, b1), (2, b2)):
                act.dma_start(bias_rows[l][:, :], b.rearrange("(a d) -> a d", a=1).broadcast_to([P, D]))\
                    .then_inc(consts_loaded, 16)
            with nc.allow_non_contiguous_dma(reason="128 numbers"):
                act.dma_start(bcol[:, :], b2.rearrange("(d a) -> d a", a=1)).then_inc(consts_loaded, 16)

            def keep_piece(s, m, t):
                n = (s * PARTS + m) * TILES + t
                act.wait_ge(piece_turned, n + 1)
                if t == 0 and not (isinstance(s, int) and s == 0):
                    act.wait_ge(pair_made, ((s - 1) * PARTS + m + 1) * CHUNKS)
                    act.wait_ge(mask_saved[m], 16 * s)
                nc.scalar.activation(halves[:, m, t, :], ps[:, 4 + t, :].bitcast(U16), ACT.Copy)\
                    .then_inc(piece_kept, 1)

            def turned(l, s, where, bank, static):
                act.wait_ge(x_turned, (l + 1) * S + s + 1)
                if not static:
                    if not (isinstance(s, int) and s == 0 and l == 0):
                        act.wait_ge(xt_kept, l * S + s)
                        act.wait_ge(t_summed, (l + 1) * S + s)
                nc.scalar.activation(where, bank, ACT.Copy, accum_out=xsum[:, bass.ds(s, 1)]).then_inc(xt_new, 1)

            def keep_t(l, s, bank):
                act.wait_ge(t_summed, (l + 1) * S + s + 1)
                nc.scalar.activation(tcol[:, bass.ds(TILES * s, TILES)], bank, ACT.Copy).then_inc(t_kept, 1)

            for s in range(S):
                turned(-1, s, XT[:, W * s:W * (s + 1)], ps[:, 4 + s % 2, :], True)
                if s:
                    keep_t(-1, s - 1, ps[:, 6 + (s - 1) % 2, 0:TILES])
            keep_t(-1, S - 1, ps[:, 6 + (S - 1) % 2, 0:TILES])
            for t in range(TILES):
                keep_piece(0, 0, t)

            def between(l):
                act.wait_ge(exponents_made, l + 1)
                if l != 1:
                    nc.scalar.activation(ccol[:, :], ccol[:, :], ACT.Exp)
                nc.scalar.activation(vcol[:, :], vcol[:, :], ACT.Exp).then_inc(exps_made, 1)
                act.wait_ge(mean_summed, l + 1)
                nc.scalar.activation(mean[:, :], ps[:, MEAN_BANK, 0:D], ACT.Copy).then_inc(mean_kept, 1)
                act.wait_ge(exps_made, l + 1)
                if l != 1:
                    nc.scalar.activation(y[:, :, D], vcol[:, :], ACT.Copy).then_inc(y_made, 1)
                if l:
                    for q in range(S):
                        act.wait_ge(v_summed, v_before[l] + q + 1)
                        if l == 1 and q >= 2:
                            act.wait_ge(y_made, 2 + q - 1)
                        for t in range(TILES):
                            to = yraw[:, q % 2, t, :] if l == 1 else y[:, TILES * q + t, 0:D]
                            last = nc.scalar.activation(to, ps[:, V_BANKS[q % 2], t * D:(t + 1) * D], ACT.Identity,
                                                        scale=vcol[:, TILES * q + t:TILES * q + t + 1])
                        last.then_inc(yraw_made, 1)
                if l in HAS_S:
                    for q in range(S):
                        act.wait_ge(s_read, s_before[l] + q + 1)
                        nc.scalar.activation(XT[:, W * q:W * (q + 1)], XT[:, W * q:W * (q + 1)], ACT.Exp,
                                             scale=1.0 - SLOPE[l]).then_inc(w_made, 1)

            def tail_norm(l, s):
                if l == 1:
                    act.wait_ge(pair_free, RING + (l * S + s + 1) * NC)
                    if not (isinstance(s, int) and s == 0):
                        act.wait_ge(sums_read, l * S + s)
                    nc.scalar.activation(low[:, :, :], sums(l, slot_of(s))[:, :, VR:VR + VC], ACT.Copy)\
                        .then_inc(low_kept, 1)
                if l == LAYERS - 1:
                    act.wait_ge(elu_asked, s + 1)
                    nc.scalar.activation(G[:, :, :], G[:, :, :], ACT.Exp).then_inc(elu_done, 1)
                act.wait_ge(norm_ready, l * S + s + 1)
                if not (isinstance(s, int) and s == 0 and l == 0):
                    act.wait_ge(x_kept, l * S + s)
                    if l < LAYERS - 1:
                        act.wait_ge(x_turned, (l + 1) * S + s)
                for t in range(TILES):
                    last = nc.scalar.activation(Xnew[:, t, :], Z[:, t, :], ACT.Identity,
                                                bias=shift[:, t:t + 1], scale=rstd[:, t:t + 1])
                last.then_inc(x_new, 1)

            def superblock(l, s, first, last):
                for m in range(PARTS):
                    if l == 0 and (m + 1 < PARTS or not last):
                        for t in range(TILES):
                            keep_piece(s if m + 1 < PARTS else s + 1, (m + 1) % PARTS, t)
                    if m == 1 and not first:
                        tail_norm(l, s - 1)
                    if m == PARTS - 2 and not first and l < LAYERS - 1:
                        turned(l, s - 1, XTnew[:, :].rearrange("p (t i) -> p t i", t=TILES),
                               sums(l, slot_of(s - 1))[:, :, 0:P], False)
                if not first and l < LAYERS - 1:
                    keep_t(l, s - 1, sums(l, slot_of(s - 1))[:, :, 250])

            for l in range(LAYERS):
                between(l)
                superblock(l, 0, True, False)
                with act.Fori(1, S - 1) as s:
                    superblock(l, s, False, False)
                superblock(l, S - 1, False, True)
                tail_norm(l, S - 1)
                if l < LAYERS - 1:
                    turned(l, S - 1, XTnew[:, :].rearrange("p (t i) -> p t i", t=TILES),
                           sums(l, slot_of(S - 1))[:, :, 0:P], False)
                    keep_t(l, S - 1, sums(l, slot_of(S - 1))[:, :, 250])

        @block.tensor
        def _(pe):
            pe.sem_inc(pair_free, RING)
            pe.wait_ge(ident_made, 2)
            pe.wait_ge(consts_loaded, 16 * 10)
            for l in (1, 2, 3):
                if l > 1:
                    pe.wait_ge(w_turn_kept, l - 1)
                pe.transpose(ps[:, 0, 0:P], Wl[l][:, :], ident[:, :]).then_inc(w_turned, 1)
                pe.wait_ge(w_turn_kept, l)
                if l > 1:
                    pe.wait_ge(wa_kept, l - 1)
                pe.matmul(ps[:, 1, 0:2], WT[:, :], acol[l][:, :], start=True, stop=True).then_inc(wa_summed, 1)
            pe.wait_ge(wa_kept, 3)
            pe.wait_ge(fills_made, 4)
            pe.matmul(ps[:, 1, 0:2], bcols[:, :], acol[2][:, :], start=True, stop=True).then_inc(wa_summed, 1)

            def turn_x(l, s, tiles, to):
                for t in range(TILES):
                    last = pe.transpose(to[:, t, 0:P], tiles[:, t, :], ident[:, :])
                last.then_inc(x_turned, 1)

            def sum_t(l, s, xt, to):
                pe.wait_ge(xt_new, (l + 1) * S + s + 1)
                for t in range(TILES):
                    last = pe.matmul(to[:, t:t + 1], xt[:, t * P:(t + 1) * P], Wa[l + 1][:, 1:2],
                                     start=True, stop=True)
                last.then_inc(t_summed, 1)

            pe.wait_ge(x_loaded, 16 * 4)
            for s in range(S + 1):
                if s < S:
                    if s >= 2:
                        pe.wait_ge(xt_new, s - 1)
                    turn_x(-1, s, X[:, TILES * s:TILES * (s + 1), :],
                           ps[:, 4 + s % 2, :].rearrange("p (t i) -> p t i", t=TILES))
                if s:
                    if s >= 3:
                        pe.wait_ge(t_kept, s - 2)
                    sum_t(-1, s - 1, XT[:, W * (s - 1):W * s], ps[:, 6 + (s - 1) % 2, :])

            def turn_piece(s, m, t):
                n = (s * PARTS + m) * TILES + t
                pe.wait_ge(piece_compared, n + 1)
                if not (isinstance(n, int) and n < TILES):
                    pe.wait_ge(piece_kept, n - (TILES - 1))
                for c in range(CHUNKS):
                    last = pe.transpose(ps[:, 4 + t, :].bitcast(BF16)[:, c * P:(c + 1) * P],
                                        bytes16[:, t, c * P:(c + 1) * P], ident16[:, :])
                last.then_inc(piece_turned, 1)

            pe.wait_ge(t_kept, S)
            for t in range(TILES):
                turn_piece(0, 0, t)

            def between(l):
                pe.wait_ge(xrows_made, l + 1)
                pe.matmul(ps[:, MEAN_BANK, 0:D], xrows[:, :], Wl[l][:, :] if l else ident[:, :],
                          start=True, stop=True).then_inc(mean_summed, 1)
                if l:
                    for q in range(S):
                        pe.wait_ge(xt_kept, l * S)
                        if q >= 2:
                            pe.wait_ge(yraw_made, v_before[l] + q - 1)
                        for t in range(TILES):
                            k = TILES * q + t
                            last = pe.matmul(ps[:, V_BANKS[q % 2], t * D:(t + 1) * D], XT[:, k * P:(k + 1) * P],
                                             Wl[l][:, :], start=True, stop=True)
                        last.then_inc(v_summed, 1)
                if l in HAS_S:
                    pe.wait_ge(wsrc_made, 3)
                    pe.wait_ge(piece_kept, TILES)
                    for q in range(S):
                        if q >= 2:
                            pe.wait_ge(s_read, s_before[l] + q - 1)
                        pe.matmul(ps[:, S_BANKS[q % 2], :], Wsrc[l][:, :], XT[:, W * q:W * (q + 1)],
                                  start=True, stop=True).then_inc(s_summed, 1)
                pe.wait_ge(y_made, [2, 2 + S, 3 + S, 4 + S][l])
                if l:
                    pe.wait_ge(yraw_made, v_before[l] + S)
                pe.wait_ge(mean_kept, l + 1)

            def step(l, s, slot, c, ring, last=False):
                pe.wait_ge(pair_made, (l * S + s) * NC + c + 1)
                to = sums(l, slot)
                for b in range(2):
                    j = bass.ds(c * 2 + b, 1)
                    if l == 1:
                        values = y_r[:, j, :, :].rearrange("p a r e -> p (a r e)")
                    else:
                        values = y[:, j, :].rearrange("p a e -> p (a e)")
                    for t in range(TILES):
                        weights = (pair_r if l == 1 else pair)[:, ring, b, t * P:(t + 1) * P]
                        mm = pe.matmul(to[:, t, 0:2 * VR if l == 1 else VC], weights, values,
                                       start=False, stop=last and b == 1, skip_group_check=True)
                mm.then_inc(pair_free, 1)

            def superblock(l, s, slot, first, last):
                if not (isinstance(s, int) and s < 2):
                    if l < LAYERS - 1:
                        pe.wait_ge(t_kept, (l + 1) * S + s - 1)
                    else:
                        pe.wait_ge(sums_read, l * S + s - 1)
                for k in range(4 if l == 1 else 2):
                    if l == 1:
                        bank, n = sums(l, slot)[:, k, 0:2 * VR], 2 * VR
                    else:
                        bank, n = sums(l, slot)[:, 2 * k:2 * k + 2, 0:VC], 2 * VC
                    pe.matmul(bank, zeros[:, 0:P], zeros[:, 0:n], start=True, stop=False, skip_group_check=True)
                for m in range(PARTS):
                    end = m == PARTS - 1
                    behind = end and not first and l < LAYERS - 1
                    if behind:
                        pe.wait_ge(x_new, l * S + s)
                        pe.wait_ge(sums_read, l * S + s)
                        turn_x(l, s - 1, Xnew[:, :, :], sums(l, 1 - slot))
                    if l <= 1 or end:
                        for c in range(CHUNKS):
                            step(l, s, slot, CHUNKS * m + c, c % RING, last=end and c == CHUNKS - 1)
                            if l == 0 and c < TILES and (not end or not last):
                                turn_piece(s if not end else s + 1, (m + 1) % PARTS, c)
                            if behind and c == CHUNKS // 2 - 1:
                                sum_t(l, s - 1, XTnew, sums(l, 1 - slot)[:, :, 250])
                    else:
                        with pe.Fori(0, CHUNKS // RING) as h:
                            for c in range(RING):
                                step(l, s, slot, CHUNKS * m + h * RING + c, c)

            for l in range(LAYERS):
                between(l)
                superblock(l, 0, 0, True, False)
                with pe.Fori(1, S - 1, 2) as s:
                    superblock(l, s, 1, False, False)
                    superblock(l, s + 1, 0, False, False)
                superblock(l, S - 1, 1, False, True)
                if l < LAYERS - 1:
                    pe.wait_ge(x_new, (l + 1) * S)
                    pe.wait_ge(sums_read, (l + 1) * S)
                    turn_x(l, S - 1, Xnew[:, :, :], sums(l, 1))
                    sum_t(l, S - 1, XTnew, sums(l, 1)[:, :, 250])

        @block.vector
        def _(dve):
            chain = Chain(dve, vec_step)
            nc.vector.memset(ones[:, :], 1.0).then_inc(fills_made, 1)
            nc.vector.memset(zeros[:, :], 0.0).then_inc(fills_made, 1)

            def compare_piece(s, m, t):
                n = (s * PARTS + m) * TILES + t
                dve.wait_ge(adj_loaded[t], 16 * (s * PARTS + m + 1))
                if not (isinstance(n, int) and n < TILES):
                    dve.wait_ge(piece_turned, n - (TILES - 1))
                nc.vector.tensor_scalar(bytes_in[:, t, :], adj_in[:, t, :], 0.0, None, ALU.is_gt)\
                    .then_inc(piece_compared, 1)

            dve.wait_ge(consts_loaded, 16 * 10)
            dve.wait_ge(fills_made, 2)
            nc.vector.tensor_scalar(bcols[:, :], ones[:, :], bcol[:, 0:1], None, ALU.mult).then_inc(fills_made, 1)
            nc.vector.memset(beta[:, :], 0.0).then_inc(fills_made, 1)
            for t in range(2):
                compare_piece(0, 0, t)
            for l in (1, 2, 3):
                dve.wait_ge(w_turned, l)
                if l > 1:
                    dve.wait_ge(wa_summed, l - 1)
                nc.vector.tensor_copy(WT[:, :], ps[:, 0, 0:P]).then_inc(w_turn_kept, 1)
                dve.wait_ge(wa_summed, l)
                nc.vector.tensor_copy(Wa[l][:, :], ps[:, 1, 0:2]).then_inc(wa_kept, 1)
            dve.wait_ge(wa_kept, 3)
            for l in HAS_S:
                nc.vector.tensor_scalar(Wsrc[l][:, :], ones[:, :], Wa[l][:, 0:1], None, ALU.mult)\
                    .then_inc(wsrc_made, 1)
            dve.wait_ge(wa_summed, 4)
            dve.wait_ge(fills_made, 4)
            chain.then(nc.vector.tensor_copy(bdot[:, :], ps[:, 1, 0:2]))
            chain.then(nc.vector.tensor_tensor(beta[:, :], bdot[:, 0:1], bdot[:, 1:2], ALU.add))
            for t in range(2, TILES):
                compare_piece(0, 0, t)

            def between(l):
                dve.wait_ge(t_kept, (l + 1) * S)
                nc.vector.tensor_reduce(tpart[:, :], tcol[:, :], AX.X, ALU.max).then_inc(tpart_made, 1)
                dve.wait_ge(xt_new, (l + 1) * S)
                chain.then(nc.vector.tensor_reduce(xtot[:, :], xsum[:, :], AX.X, ALU.add))
                if l:
                    dve.wait_ge(mean_summed, l)
                nc.vector.tensor_scalar(xrows[:, :], ones[:, :], xtot[:, 0:1], 1.0 / N, ALU.mult, ALU.mult)\
                    .then_inc(xrows_made, 1)
                dve.wait_ge(tmax_made, l + 1)
                chain.then(nc.vector.tensor_scalar(tcol[:, :], tcol[:, :], tmax[:, 0:1], None, ALU.subtract))
                if l != 1:
                    chain.then(nc.vector.tensor_scalar(ccol[:, :], tcol[:, :], -(1.0 - SLOPE[l]), CAP,
                                                       ALU.mult, ALU.min))
                    if l == 2:
                        chain.then(nc.vector.tensor_tensor(sbias[:, :], tmax[:, :], beta[:, :], ALU.add))
                nc.vector.tensor_scalar(vcol[:, :], tcol[:, :], KAPPA, None, ALU.subtract)\
                    .then_inc(exponents_made, 1)
                dve.wait_ge(exps_made, l + 1)
                if l == 0:
                    nc.vector.tensor_tensor(y[:, :, 0:D], X[:, :, :],
                                            vcol[:, :].rearrange("p (q a) -> p q a", a=1).broadcast_to([P, NB, D]),
                                            ALU.mult).then_inc(y_made, 1)
                if l == 1:
                    y32 = y_r[:, :, :, :].bitcast(F32)
                    v3 = vcol[:, :].rearrange("p (q a) -> p q a", a=1)
                    chain.then(nc.vector.tensor_copy(y_r[:, :, 0, D:D + 1], v3))
                    nc.vector.tensor_tensor(y_r[:, :, 1, D:D + 1], v3, y32[:, :, 0, D:D + 1], ALU.subtract)
                    for r in range(2):
                        chain.then(nc.vector.tensor_scalar(y_r[:, :, r, D + 1:D + 2], v3, 0.0, None, ALU.mult))
                    for q in range(S):
                        dve.wait_ge(yraw_made, v_before[l] + q + 1)
                        b = slice(TILES * q, TILES * (q + 1))
                        chain.then(nc.vector.tensor_copy(y_r[:, b, 0, 0:D], yraw[:, q % 2, :, :]))
                        nc.vector.tensor_tensor(y_r[:, b, 1, 0:D], yraw[:, q % 2, :, :], y32[:, b, 0, 0:D],
                                                ALU.subtract).then_inc(y_made, 1)
                if l in HAS_S:
                    guard = sbias if l == 2 else tmax
                    for q in range(S):
                        dve.wait_ge(s_summed, s_before[l] + q + 1)
                        nc.vector.tensor_scalar(XT[:, W * q:W * (q + 1)], ps[:, S_BANKS[q % 2], :], guard[:, 0:1],
                                                CAP / (1.0 - SLOPE[l]), ALU.add, ALU.min).then_inc(s_read, 1)
                    dve.wait_ge(w_made, s_before[l] + S)
                dve.wait_ge(mean_kept, l + 1)

            def step(l, s, m, c, ring):
                dve.wait_ge(pair_free, (l * S + s) * NC + CHUNKS * m + c + 1)
                for b in range(2):
                    bits = pairs[:, m, :, bass.ds(c, 1), :, b].rearrange("p t c i -> p t (c i)")
                    to = (pair_r if l == 1 else pair)[:, ring, b, :].rearrange("p (t i) -> p t i", t=TILES)
                    if l == 1:
                        made = nc.vector.tensor_copy(to, bits)
                    else:
                        made = nc.vector.scalar_tensor_tensor(
                            to, XT[:, bass.ds(s * W, W)].rearrange("p (t i) -> p t i", t=TILES),
                            ccol[:, bass.ds(PB * m + c * 2 + b, 1)], bits, ALU.max, ALU.mult)
                made.then_inc(pair_made, 1)

            def tail(l, s, base):
                chain.at = base
                old = X[:, bass.ds(TILES * s, TILES), :]
                got = sums(l, slot_of(s))
                dve.wait_ge(pair_free, RING + (l * S + s + 1) * NC)
                if l == 1:
                    dve.wait_ge(low_kept, s + 1)
                    chain.then(nc.vector.tensor_tensor(low[:, :, :], got[:, :, 0:VC], low[:, :, :], ALU.add))
                    got = low
                    yield
                chain.then(nc.vector.tensor_scalar(flag[:, :], got[:, :, D], 0.0, None, ALU.is_equal))
                chain.then(nc.vector.tensor_tensor(den[:, :], got[:, :, D], flag[:, :], ALU.add))
                chain.then(nc.vector.reciprocal(rinv[:, :], den[:, :]))
                yield
                if not (isinstance(s, int) and s == 0 and l == 0):
                    dve.wait_ge(x_new, l * S + s)
                for t in range(TILES):
                    if l < LAYERS - 1:
                        g = nc.vector.scalar_tensor_tensor(G[:, t, :], mean[:, :], flag[:, t:t + 1],
                                                           X[:, bass.ds(TILES * s + t, 1), :].rearrange("p a d -> p (a d)"),
                                                           ALU.mult, ALU.add)
                    else:
                        g = nc.vector.tensor_scalar(G[:, t, :], mean[:, :], flag[:, t:t + 1], None, ALU.mult)
                chain.then(g)
                yield
                for t in range(TILES):
                    z = nc.vector.scalar_tensor_tensor(Z[:, t, :], got[:, t, 0:D], rinv[:, t:t + 1], G[:, t, :],
                                                       ALU.mult, ALU.add)
                z.then_inc(sums_read, 1)
                dve.wait_ge(sums_read, l * S + s + 1)
                yield
                if l in bias_rows:
                    chain.then(nc.vector.tensor_tensor(
                        Z[:, :, :], Z[:, :, :],
                        bias_rows[l][:, :].rearrange("p (a d) -> p a d", a=1).broadcast_to([P, TILES, D]), ALU.add))
                    yield
                if l == LAYERS - 1:
                    nc.vector.tensor_scalar(G[:, :, :], Z[:, :, :], 0.0, None, ALU.min).then_inc(elu_asked, 1)
                    chain.then(nc.vector.tensor_scalar(Z[:, :, :], Z[:, :, :], 0.0, None, ALU.max))
                    yield
                    dve.wait_ge(elu_done, s + 1)
                    chain.then(nc.vector.scalar_tensor_tensor(Z[:, :, :], G[:, :, :], -1.0, Z[:, :, :],
                                                              ALU.add, ALU.add))
                    yield
                    chain.then(nc.vector.tensor_tensor(Z[:, :, :], Z[:, :, :], old, ALU.add))
                    yield
                for t in range(TILES):
                    b = nc.vector.bn_stats(stats[:, t, :], Z[:, t, :])
                chain.then(b)
                yield
                dve.sem_inc(dve_waited, 1)
                for t in range(TILES):
                    b = nc.vector.bn_aggr(mv[:, t, :], stats[:, t, :])
                chain.then(b)
                nc.vector.tensor_scalar(spread[:, :], mv[:, :, 1], EPS, None, ALU.add).then_inc(moments_made, 1)
                nc.vector.tensor_scalar(minus[:, :], mv[:, :, 0], -1.0, None, ALU.mult).then_inc(moments_made, 1)

            def superblock(l, s, first, last, base):
                for m in range(PARTS):
                    loaded = (piece_kept, TILES * (s * PARTS + m + 1)) if l == 0 else \
                        (mask_loaded[m], 16 * ((l - 1) * S + s + 1))
                    behind = not first and m == 1
                    if behind:
                        stages = tail(l, s - 1, base + (s - 1) * TAIL[l])
                    if l == 0 or behind:
                        dve.wait_ge(*loaded)
                        for c in range(CHUNKS):
                            if l == 0 and c < TILES and (m + 1 < PARTS or not last):
                                compare_piece(s if m + 1 < PARTS else s + 1, (m + 1) % PARTS, c)
                            step(l, s, m, c, c % RING)
                            if behind:
                                next(stages, None)
                        if behind:
                            assert next(stages, 0) == 0
                    else:
                        with dve.Fori(0, CHUNKS // RING) as h:
                            dve.wait_ge(*loaded)
                            for c in range(RING):
                                step(l, s, m, h * RING + c, c)

            for l in range(LAYERS):
                between(l)
                base = chain.at
                superblock(l, 0, True, False, base)
                with dve.Fori(1, S - 1) as s:
                    superblock(l, s, False, False, base)
                superblock(l, S - 1, False, True, base)
                at = base + (S - 1) * TAIL[l]
                assert chain.at == at, (l, base, chain.at, at)
                for _ in tail(l, S - 1, at):
                    pass


_INS = ["x", "adj", "L0_gnn_a", "L1_gnn_W_fc", "L1_gnn_b_fc", "L1_gnn_w_att", "L2_gnn_W_w", "L2_gnn_W_b",
        "L2_gnn_a", "L3_gnn_W", "L3_gnn_a"]


def kernel(**inputs):
    import numpy as _np
    import concourse.bacc as _bacc
    from concourse import mybir as _mybir
    from concourse.bass_utils import run_bass_kernel_spmd as _run

    nc = _bacc.Bacc("TRN2", target_bir_lowering=False, num_devices=1)
    arrays, args = {}, []
    for name in _INS:
        a = _np.ascontiguousarray(inputs[name])
        if name.endswith("_a"):
            a = a.reshape(-1)
        arrays[f"in_{name}_dram"] = a
        args.append(nc.dram_tensor(f"in_{name}_dram", a.shape, _mybir.dt.from_np(a.dtype), kind="ExternalInput").ap())
    n, d = inputs["x"].shape
    args.append(nc.dram_tensor("out_0_dram", (n, d), _mybir.dt.float32, kind="ExternalOutput").ap())
    gat4(nc, *args)
    r = _run(nc, [arrays], core_ids=[0])
    return r.results[0]["out_0_dram"]
```

```python
from contextlib import ExitStack

import concourse.bass as bass
from concourse import mybir

P = 128
D = 128
TILES = 4
W = TILES * P
CHUNKS = 8
PB = 2 * CHUNKS
PCOLS = PB * P
RING = 8
LAYERS = 4
AHEAD = 1
SLOPE = [0.01, None, 0.2, 0.2]
EPS = 1e-5
KAPPA = 8.0
CAP = 78.0
VC = D + 1
DL = D - 1

ALU = mybir.AluOpType
ACT = mybir.ActivationFunctionType
AX = mybir.AxisListType
F32 = mybir.dt.float32
F32R = mybir.dt.float32r
BF16 = mybir.dt.bfloat16
U8 = mybir.dt.uint8
U16 = mybir.dt.uint16
I32 = mybir.dt.int32
RMAX = bass.bass_isa.ReduceOp.max


class Chain:

    def __init__(self, engine, semaphore):
        self.engine, self.semaphore, self.at = engine, semaphore, 0

    def then(self, instruction):
        instruction.then_inc(self.semaphore, 1)
        self.at = self.at + 1
        self.engine.wait_ge(self.semaphore, self.at)


def gat4(nc, x, adj, a0, w1, b1, a1, w2, b2, a2, w3, a3, out):
    N = x.shape[0]
    NB = N // P
    S = NB // TILES
    PARTS = NB // PB
    NC = NB // 2

    TAIL = [6, 6, 6, 9]

    with ExitStack() as ctx:
        def sb(name, shape, dt, stack=ctx):
            return stack.enter_context(nc.sbuf_tensor(name, shape, dt))

        def sem(name):
            return ctx.enter_context(nc.semaphore(name))

        X = sb("X", [P, NB, D], F32)
        w_rows = sb("w_rows", [P, 2, W], F32)
        mask = sb("mask", [P, PARTS, TILES * PCOLS], U8)
        ident = sb("ident", [P, P], F32)
        ident16 = sb("ident16", [P, P], BF16)
        ones = sb("ones", [P, P], F32)
        zeros = sb("zeros", [P, W], BF16)
        Wl = {1: sb("W1", [P, D], F32), 2: sb("W2", [P, D], F32), 3: sb("W3", [P, D], F32)}
        acol = {l: sb(f"acol{l}", [P, 2], F32) for l in (1, 2, 3)}
        arows = {l: sb(f"arows{l}", [P, 2, D], F32) for l in (1, 2, 3)}
        Wnat = {l: sb(f"Wnat{l}", [P, VC], F32) for l in (1, 2, 3)}
        bias_rows = {1: sb("bias1", [P, D], F32), 2: sb("bias2", [P, D], F32)}
        bcol = sb("bcol", [P, 1], F32)
        bdot = sb("bdot", [P, 2], F32)
        beta = sb("beta", [P, 1], F32)
        scores = sb("scores", [P, NB, 2], F32)
        tcol = sb("tcol", [P, NB], F32)
        wcol = sb("wcol", [P, NB], F32)
        w_diag = sb("w_diag", [P, TILES, P], F32)
        tpart = sb("tpart", [P, 1], F32)
        tmax = sb("tmax", [P, 1], F32)
        sbias = sb("sbias", [P, 1], F32)
        ccol = sb("ccol", [P, NB], F32)
        vcol = sb("vcol", [P, NB], F32)
        xsums = sb("xsums", [P, TILES, D], F32)
        xtot = sb("xtot", [P, 1], F32)
        xrows = sb("xrows", [P, P], F32)
        mean = sb("mean", [P, D], F32)
        flag = sb("flag", [P, TILES], F32)
        den = sb("den", [P, TILES], F32)
        rinv = sb("rinv", [P, TILES], F32)
        G = sb("G", [P, TILES, D], F32)
        Z = sb("Z", [P, TILES, D], F32)
        stats = sb("stats", [P, TILES, 6], F32)
        mv = sb("mv", [P, TILES, 2], F32)
        spread = sb("spread", [P, TILES], F32)
        minus = sb("minus", [P, TILES], F32)
        power = sb("power", [P, TILES], F32)
        rstd = sb("rstd", [P, TILES], F32)
        shift = sb("shift", [P, TILES], F32)
        Xnew = sb("Xnew", [P, TILES, D], F32)

        aggr = sb("aggr", [P, W], F32)

        with ExitStack() as stack:
            pair = sb("pair", [P, RING, 2, W], F32, stack)
            y = sb("y", [P, NB, VC], F32, stack)
            arows[0] = sb("arows0", [P, 2, D], F32, stack)
            avec = sb("avec", [P, 2, P], F32, stack)
            WT = sb("WT", [P, D], F32, stack)
            bcols = sb("bcols", [P, P], F32, stack)
            adj_in = sb("adj_in", [P, TILES, PCOLS], I32, stack)
            bytes_in = sb("bytes_in", [P, TILES, PCOLS], U8, stack)
        with ExitStack() as stack:
            bits_r = sb("bits_r", [P, RING, 2, W], F32R, stack)
            y1_r = sb("y1_r", [P, NB, 2, D], F32R, stack)
            y1_raw = sb("y1_raw", [P, 2, TILES, D], F32, stack)
        full = sb("full", [P, RING, W], F32)
        split = sb("split", [P, RING, W], F32)
        split_hi = sb("split_hi", [P, RING, W], F32R)
        split_lo = sb("split_lo", [P, RING, W], F32R)
        y_full = sb("y_full", [P, NC, D], F32)
        y_split_r = sb("y_split_r", [P, NC, 2, D], F32R)
        y_split_raw = sb("y_split_raw", [P, 2, 2, D], F32)

        ps = ctx.enter_context(nc.psum_tensor("ps", [P, 8, 512], F32))
        scratch = nc.dram_tensor("mask_scratch", (S, PARTS, P, TILES * PCOLS), U8, kind="Internal").ap()

        x_loaded = [sem(f"x_loaded{k}") for k in range(4)]
        consts_loaded = sem("consts_loaded")
        scores_loaded = sem("scores_loaded")
        adj_loaded = [sem(f"adj_loaded{t}") for t in range(TILES)]
        mask_saved = [sem(f"mask_saved{m}") for m in range(PARTS)]
        mask_loaded = [sem(f"mask_loaded{m}") for m in range(PARTS)]
        ident_zeroed = sem("ident_zeroed")
        ident_made = sem("ident_made")
        fills_made = sem("fills_made")
        w_turned = sem("w_turned")
        w_turn_kept = sem("w_turn_kept")
        avec_made = sem("avec_made")
        arows_summed = sem("arows_summed")
        arows_kept = sem("arows_kept")
        bias_scored = sem("bias_scored")
        wnat_made = sem("wnat_made")
        piece_positive = sem("piece_positive")
        piece_compared = sem("piece_compared")
        piece_signed = sem("piece_signed")
        piece_turned = sem("piece_turned")
        piece_kept = sem("piece_kept")
        pair_made = sem("pair_made")
        pair_free = sem("pair_free")
        full_made = sem("full_made")
        full_free = sem("full_free")
        split_made = sem("split_made")
        high_made = sem("high_made")
        low_made = sem("low_made")
        split_free = sem("split_free")
        aggr_kept = sem("aggr_kept")
        rows_summed = sem("rows_summed")
        sums_read = sem("sums_read")
        elu_asked = sem("elu_asked")
        elu_done = sem("elu_done")
        moments_made = sem("moments_made")
        rstd_made = sem("rstd_made")
        norm_ready = sem("norm_ready")
        x_new = sem("x_new")
        x_kept = sem("x_kept")
        scored = sem("scored")
        x_added = sem("x_added")
        tpart_made = sem("tpart_made")
        tmax_made = sem("tmax_made")
        exponents_made = sem("exponents_made")
        exps_made = sem("exps_made")
        xsums_zeroed = sem("xsums_zeroed")
        x_summed = sem("x_summed")
        xrows_made = sem("xrows_made")
        mean_summed = sem("mean_summed")
        mean_kept = sem("mean_kept")
        y_full_made = sem("y_full_made")
        y_raw_made = sem("y_raw_made")
        y_high_made = sem("y_high_made")
        y0_made = sem("y0_made")
        y0_more = sem("y0_more")
        y_made = sem("y_made")
        s_scored = sem("s_scored")
        w_asked = sem("w_asked")
        w_made = sem("w_made")
        diag_made = sem("diag_made")
        w_spread = sem("w_spread")
        w_kept = sem("w_kept")
        vec_step = sem("vec_step")
        dve_waited = sem("dve_waited")
        act_waited = sem("act_waited")
        sp_waited = sem("sp_waited")

        x_v = x.rearrange("(c p b) d -> p c (b d)", p=P, b=2)
        out_v = out.rearrange("(s h p b) d -> s p h (b d)", h=2, p=P, b=2)
        adj_v = adj.rearrange("(s h p b) (m j) -> s h b m p j", h=2, p=P, b=2, m=PARTS)
        words = mask[:, :, :].bitcast(I32)
        halves = mask[:, :, :].rearrange("p m (t w) -> p m t w", t=TILES).bitcast(U16)
        pairs = mask[:, :, :].rearrange("p m (t c i b) -> p m t c i b", t=TILES, c=CHUNKS, b=2)
        bytes16 = bytes_in[:, :, :].bitcast(BF16)

        def sums0(slot):
            return ps[:, bass.ds(2 * slot, 2), :].rearrange("p k (t e) -> p (k t) e", t=2)

        def sumsT(slot):
            return ps[:, bass.ds(slot, 1), :].rearrange("p k i -> p (k i)")

        NAT = ps[:, 2:4, :].rearrange("p k (t e) -> p (k t) e", t=2)
        X_SUM = ps[:, 3, 0:1]
        MEAN_BANK = 0
        HAS_S = (0, 2, 3)
        s_before = {l: sum(S for k in HAS_S if k < l) for l in range(LAYERS)}

        def natural(l, slot):
            return sums0(slot) if l == 0 else NAT

        def w_bank(l, s):
            return 6 if l else 1 if isinstance(s, int) and s == 0 else 4

        def w_count(l, s):
            return s_before[l] + s

        def split_count(l, s, c):
            return ((l - 2) * S + s) * NC + c

        def y_count(l, q):
            return (l - 1) * S + q

        block = ctx.enter_context(nc.Block())

        @block.sync
        def _(sp):
            def load_piece(s, m, t):
                g = s * PARTS + m
                if not (isinstance(g, int) and g == 0):
                    if t == TILES - 1:
                        sp.wait_ge(piece_signed, g)
                    else:
                        sp.wait_ge(piece_compared, (g - 1) * (TILES - 1) + t + 1)
                sp.dma_start(adj_in[:, t, :], adj_v[s, t // 2, t % 2, m]).then_inc(adj_loaded[t], 16)

            xq = NB // 2 // 4
            for k in range(4):
                sp.dma_start(X[:, 2 * xq * k:2 * xq * (k + 1), :].rearrange("p (c b) d -> p c (b d)", b=2),
                             x_v[:, xq * k:xq * (k + 1), :]).then_inc(x_loaded[k], 16)
            for t in range(TILES):
                load_piece(0, 0, t)

            def superblock0(s, last):
                for m in range(PARTS):
                    for t in range(TILES):
                        if m + 1 < PARTS:
                            load_piece(s, m + 1, t)
                        elif not last:
                            load_piece(s + 1, 0, t)
                    sp.wait_ge(piece_kept, TILES * (s * PARTS + m + 1))
                    sp.sem_inc(sp_waited, 1)
                    sp.dma_start(scratch[s, m].bitcast(I32), words[:, m, :]).then_inc(mask_saved[m], 16)

            with sp.Fori(0, S - 1) as s:
                superblock0(s, False)
            superblock0(S - 1, True)

            def load_part(l, s, m):
                if l == 1 or (l == 2 and isinstance(s, int)):
                    sp.wait_ge(pair_made, ((l * S + s - 1) * PARTS + m + 1) * CHUNKS)
                else:
                    sp.wait_ge(split_made, split_count(l, s - 1, CHUNKS * (m + 1)))
                sp.sem_inc(sp_waited, 1)
                sp.dma_start(words[:, m, :], scratch[s, m].bitcast(I32)).then_inc(mask_loaded[m], 16)

            for l in range(1, LAYERS):
                for m in range(PARTS):
                    sp.wait_ge(mask_saved[m], 16 * S)
                    load_part(l, 0, m)
                with sp.Fori(1, S) as s:
                    for m in range(PARTS):
                        load_part(l, s, m)

        @block.gpsimd
        def _(pool):
            nc.gpsimd.memset(ident[:, :], 0.0).then_inc(ident_zeroed, 1)
            nc.gpsimd.memset(ident16[:, :], 0.0).then_inc(ident_zeroed, 1)
            nc.gpsimd.memset(power[:, :], -0.5).then_inc(ident_zeroed, 1)
            pool.wait_ge(ident_zeroed, 3)
            for i in (ident, ident16):
                nc.gpsimd.affine_select(out=i[:, :], in_=i[:, :], compare_op=ALU.not_equal, fill=1.0, base=0,
                                        pattern=[[-1, P]], channel_multiplier=1).then_inc(ident_made, 1)

            pool.sem_inc(low_made, RING)

            def norm(l, s):
                pool.wait_ge(moments_made, 2 * (l * S + s + 1))
                nc.gpsimd.tensor_tensor(rstd[:, :], spread[:, :], power[:, :], ALU.pow).then_inc(rstd_made, 1)
                pool.wait_ge(rstd_made, l * S + s + 1)
                nc.gpsimd.tensor_tensor(shift[:, :], minus[:, :], rstd[:, :], ALU.mult).then_inc(norm_ready, 1)

            def add_x(l, s, rows):
                n = (l + 1) * S + s
                pool.wait_ge(x_added, n) if not (isinstance(n, int) and n == 0) else None
                nc.gpsimd.tensor_tensor(xsums[:, :, :], xsums[:, :, :], rows, ALU.add).then_inc(x_added, 1)

            def add_new(l, s):
                pool.wait_ge(x_new, l * S + s + 1)
                add_x(l, s, Xnew[:, :, :])

            def zero_sums(l):
                pool.wait_ge(x_summed, l + 1)
                nc.gpsimd.memset(xsums[:, :, :], 0.0).then_inc(xsums_zeroed, 1)
                pool.wait_ge(xsums_zeroed, l + 2)

            def low_weights(l, s, c):
                pool.wait_ge(high_made, split_count(l, s, c + 1))
                nc.gpsimd.tensor_tensor(split_lo[:, c % RING, :], split[:, c % RING, :],
                                        split_hi[:, c % RING, :].bitcast(F32), ALU.subtract).then_inc(low_made, 1)

            def low_values(l, q):
                pool.wait_ge(y_high_made, y_count(l, q + 1))
                if l == 1:
                    b = slice(TILES * q, TILES * (q + 1))
                    nc.gpsimd.tensor_tensor(y1_r[:, b, 1, :], y1_raw[:, q % 2, :, :],
                                            y1_r[:, b, 0, :].bitcast(F32), ALU.subtract).then_inc(y_made, 1)
                else:
                    b = slice(2 * q, 2 * q + 2)
                    nc.gpsimd.tensor_tensor(y_split_r[:, b, 1, :], y_split_raw[:, q % 2, :, :],
                                            y_split_r[:, b, 0, :].bitcast(F32), ALU.subtract).then_inc(y_made, 1)

            def superblock(l, s, first):
                for c in range(NC):
                    low_weights(l, s, c)
                    if first and c % 2 == 1 and c // 2 + AHEAD < S:
                        low_values(l, c // 2 + AHEAD)
                    if c == 2 * CHUNKS - 1 and not first:
                        norm(l, s - 1)
                    if c == 3 * CHUNKS and not first and l < LAYERS - 1:
                        add_new(l, s - 1)

            nc.gpsimd.memset(xsums[:, :, :], 0.0).then_inc(xsums_zeroed, 1)
            pool.wait_ge(xsums_zeroed, 1)

            def add_input(q):
                pool.wait_ge(x_loaded[4 * q // S], 16)
                add_x(-1, q, X[:, TILES * q:TILES * (q + 1), :])

            for q in range(S // 2):
                add_input(q)
            for l in range(LAYERS):
                pool.wait_ge(tpart_made, l + 1)
                nc.gpsimd.partition_all_reduce(tmax[:, :], tpart[:, :], P, RMAX).then_inc(tmax_made, 1)
                if l:
                    for q in range(S if l == 1 else AHEAD):
                        low_values(l, q)
                if l == 0:
                    for q in range(S // 2, S):
                        add_input(q)
                    for m in range(1, PARTS):
                        pool.wait_ge(exps_made, 1)
                        b = slice(PB * m, PB * (m + 1))
                        nc.gpsimd.tensor_tensor(
                            y[:, b, 0:D], X[:, b, :],
                            vcol[:, b].rearrange("p (q a) -> p q a", a=1).broadcast_to([P, PB, D]),
                            ALU.mult).then_inc(y0_more, 1)
                if l < LAYERS - 1:
                    zero_sums(l)
                if l < 2:
                    with pool.Fori(0, S) as s:
                        norm(l, s)
                        add_new(l, s)
                else:
                    superblock(l, 0, True)
                    with pool.Fori(1, S) as s:
                        superblock(l, s, False)
                    norm(l, S - 1)
                    if l < LAYERS - 1:
                        add_new(l, S - 1)

        @block.scalar
        def _(act):
            act.sem_inc(x_kept, 16)
            act.dma_start(arows[0][:, :, :].rearrange("p h k -> p (h k)"),
                          a0.rearrange("(a k) -> a k", a=1).broadcast_to([P, 2 * D])).then_inc(scores_loaded, 16)
            for l, a in ((1, a1), (2, a2), (3, a3)):
                with nc.allow_non_contiguous_dma(reason="256 numbers"):
                    act.dma_start(acol[l][:, :], a.rearrange("(h k) -> k h", h=2)).then_inc(consts_loaded, 16)
            for l, w in ((1, w1), (2, w2), (3, w3)):
                act.dma_start(Wl[l][:, :], w).then_inc(consts_loaded, 16)
            for l, b in ((1, b1), (2, b2)):
                act.dma_start(bias_rows[l][:, :], b.rearrange("(a d) -> a d", a=1).broadcast_to([P, D]))\
                    .then_inc(consts_loaded, 16)
            with nc.allow_non_contiguous_dma(reason="128 numbers"):
                act.dma_start(bcol[:, :], b2.rearrange("(d a) -> d a", a=1)).then_inc(consts_loaded, 16)

            for l, w in ((1, w1), (2, w2), (3, w3)):
                act.dma_start(Wnat[l][:, 0:D], w[DL:D, :].broadcast_to([P, D])).then_inc(consts_loaded, 16)

            def sign_piece(s, m):
                g = s * PARTS + m
                t = TILES - 1
                act.wait_ge(adj_loaded[t], 16 * (g + 1))
                nc.scalar.activation(adj_in[:, t, :].bitcast(F32), adj_in[:, t, :], ACT.Relu)\
                    .then_inc(piece_positive, 1)
                if not (isinstance(g, int) and g == 0):
                    act.wait_ge(piece_turned, TILES * g)
                act.wait_ge(piece_positive, g + 1)
                nc.scalar.activation(bytes_in[:, t, :], adj_in[:, t, :].bitcast(F32), ACT.Sign)\
                    .then_inc(piece_signed, 1)

            def keep_piece(s, m, t):
                n = (s * PARTS + m) * TILES + t
                act.wait_ge(piece_turned, n + 1)
                if t == 0 and not (isinstance(s, int) and s == 0):
                    act.wait_ge(pair_made, ((s - 1) * PARTS + m + 1) * CHUNKS)
                    act.wait_ge(mask_saved[m], 16 * s)
                nc.scalar.activation(halves[:, m, t, :], ps[:, 4 + t, :].bitcast(U16), ACT.Copy)\
                    .then_inc(piece_kept, 1)

            def high_values(l, q):
                raw = y1_raw if l == 1 else y_split_raw
                if q >= 2:
                    act.wait_ge(y_made, y_count(l, q - 1))
                for t in range(0 if l == 1 else 1, TILES, 1 if l == 1 else 2):
                    k = TILES * q + t
                    to = raw[:, q % 2, t if l == 1 else t // 2, :]
                    nc.scalar.activation(to[:, 0:DL], X[:, k, 0:DL], ACT.Identity, scale=vcol[:, k:k + 1])
                v = vcol[:, TILES * q:TILES * (q + 1)]
                if l > 1:
                    v = v.rearrange("p (c b) -> p c b", b=2)[:, :, 1]
                nc.scalar.activation(raw[:, q % 2, :, DL], v, ACT.Copy).then_inc(y_raw_made, 1)
                act.wait_ge(y_raw_made, y_count(l, q + 1))
                to = y1_r[:, TILES * q:TILES * (q + 1), 0, :] if l == 1 else y_split_r[:, 2 * q:2 * q + 2, 0, :]
                nc.scalar.activation(to, raw[:, q % 2, :, :], ACT.Copy).then_inc(y_high_made, 1)

            def make_diag(l, s):
                n = w_count(l, s)
                if l == 0:
                    w = wcol[:, bass.ds(TILES * s, TILES)]
                    act.wait_ge(w_asked, s + 1)
                    act.sem_inc(act_waited, 1)
                    nc.scalar.activation(w, w, ACT.Exp, scale=1.0 - SLOPE[l]).then_inc(w_made, 1)
                    act.wait_ge(w_made, s + 1)
                if not (isinstance(n, int) and n == 0):
                    act.wait_ge(w_spread, n)
                act.sem_inc(act_waited, 1)
                for t in range(TILES):
                    last = nc.scalar.activation(w_diag[:, t, :], ident[:, :], ACT.Identity,
                                                scale=wcol[:, bass.ds(TILES * s + t, 1)])
                last.then_inc(diag_made, 1)

            def keep_w(l, s):
                act.wait_ge(w_spread, w_count(l, s) + 1)
                if l == 0 and not (isinstance(s, int) and s < 2):
                    act.wait_ge(pair_made, (s - 1) * NC)
                nc.scalar.activation(w_rows[:, bass.ds(s % 2, 1), :].rearrange("p a i -> p (a i)"),
                                     ps[:, w_bank(l, s), :], ACT.Copy).then_inc(w_kept, 1)

            def between(l):
                if l:
                    act.wait_ge(x_kept, 16 * (l * S + 1))
                act.wait_ge(exponents_made, l + 1)
                if l != 1:
                    nc.scalar.activation(ccol[:, :], ccol[:, :], ACT.Exp)
                    if l:
                        nc.scalar.activation(wcol[:, :], wcol[:, :], ACT.Exp, scale=1.0 - SLOPE[l])
                nc.scalar.activation(vcol[:, :], vcol[:, :], ACT.Exp).then_inc(exps_made, 1)
                act.wait_ge(exps_made, l + 1)
                if l in HAS_S:
                    make_diag(l, 0)
                if l == 0:
                    nc.scalar.activation(y[:, :, D], vcol[:, :], ACT.Copy).then_inc(y0_made, 1)
                if l in HAS_S:
                    keep_w(l, 0)
                if l == 0:
                    sign_piece(0, 0)
                    for t in range(TILES):
                        keep_piece(0, 0, t)
                act.wait_ge(mean_summed, l + 1)
                nc.scalar.activation(mean[:, :], ps[:, MEAN_BANK, 0:D], ACT.Copy).then_inc(mean_kept, 1)
                if l == 0:
                    sign_piece(0, 1)
                    return
                for q in range(S if l == 1 else AHEAD):
                    high_values(l, q)

            def keep_sums(l, s):
                if l == 1:
                    act.wait_ge(pair_free, RING + (S + s + 1) * NC)
                else:
                    act.wait_ge(split_free, RING + split_count(l, s + 1, 0))
                nc.scalar.activation(aggr[:, :], sumsT(s % 2), ACT.Copy).then_inc(aggr_kept, 1)

            def elu(s):
                act.wait_ge(elu_asked, s + 1)
                nc.scalar.activation(G[:, :, :], G[:, :, :], ACT.Exp).then_inc(elu_done, 1)

            def normalise(l, s):
                act.wait_ge(norm_ready, l * S + s + 1)
                if l < LAYERS - 1:
                    act.wait_ge(scored, (l + 1) * S + s)
                    act.wait_ge(x_added, (l + 1) * S + s)
                act.wait_ge(x_kept, 16 * (l * S + s + 1))
                for t in range(TILES):
                    last = nc.scalar.activation(Xnew[:, t, :], Z[:, t, :], ACT.Identity,
                                                bias=shift[:, t:t + 1], scale=rstd[:, t:t + 1])
                last.then_inc(x_new, 1)
                act.wait_ge(x_new, l * S + s + 1)
                if l < LAYERS - 1:
                    act.dma_start(X[:, bass.ds(TILES * s, TILES), :], Xnew[:, :, :]).then_inc(x_kept, 16)
                else:
                    act.dma_start(out_v[s], Xnew[:, :, :].rearrange("p (h b) d -> p h (b d)", b=2))\
                        .then_inc(x_kept, 16)

            def superblock0(s, first, last):
                for m in range(PARTS):
                    if m + 1 < PARTS or not last:
                        for t in range(TILES):
                            keep_piece(s if m + 1 < PARTS else s + 1, (m + 1) % PARTS, t)
                    if m + 2 < PARTS or not last:
                        sign_piece(s if m + 2 < PARTS else s + 1, (m + 2) % PARTS)
                    if m == 1 and not last:
                        make_diag(0, s + 1)
                    if m == 2 and not last:
                        keep_w(0, s + 1)
                    if m == 1 and not first:
                        normalise(0, s - 1)

            def tail(l, s):
                if l:
                    keep_sums(l, s)
                if l == LAYERS - 1:
                    elu(s)
                normalise(l, s)

            def superblock(l, s, first, last):
                for c in range(NC):
                    act.wait_ge(split_made, split_count(l, s, c + 1))
                    act.wait_ge(split_free, split_count(l, s, c + 1))
                    nc.scalar.activation(split_hi[:, c % RING, :], split[:, c % RING, :], ACT.Copy)\
                        .then_inc(high_made, 1)
                    if c == 3 and not last:
                        make_diag(l, s + 1)
                    if c == CHUNKS and not last:
                        keep_w(l, s + 1)
                    if first:
                        if c % 2 and c // 2 + AHEAD < S:
                            high_values(l, c // 2 + AHEAD)
                        continue
                    if c == 0:
                        keep_sums(l, s - 1)
                    if c == CHUNKS + 3 and l == LAYERS - 1:
                        elu(s - 1)
                    if c == 2 * CHUNKS + 2:
                        normalise(l, s - 1)

            for l in range(LAYERS):
                between(l)
                if l == 0:
                    superblock0(0, True, False)
                    with act.Fori(1, S - 1) as s:
                        superblock0(s, False, False)
                    superblock0(S - 1, False, True)
                    tail(0, S - 1)
                elif l == 1:
                    with act.Fori(0, S) as s:
                        tail(l, s)
                else:
                    superblock(l, 0, True, False)
                    with act.Fori(1, S - 1) as s:
                        superblock(l, s, False, False)
                    superblock(l, S - 1, False, True)
                    tail(l, S - 1)
            act.wait_ge(x_kept, 16 * (LAYERS * S + 1))

        @block.tensor
        def _(pe):
            pe.sem_inc(pair_free, RING)
            def turn_piece(s, m, t):
                g = s * PARTS + m
                if t == TILES - 1:
                    pe.wait_ge(piece_signed, g + 1)
                else:
                    pe.wait_ge(piece_compared, g * (TILES - 1) + t + 1)
                if not (isinstance(g, int) and g == 0):
                    pe.wait_ge(piece_kept, (g - 1) * TILES + t + 1)
                for c in range(CHUNKS):
                    last = pe.transpose(ps[:, 4 + t, :].bitcast(BF16)[:, c * P:(c + 1) * P],
                                        bytes16[:, t, c * P:(c + 1) * P], ident16[:, :])
                last.then_inc(piece_turned, 1)

            pe.wait_ge(ident_made, 2)

            def make_constants():
                pe.wait_ge(consts_loaded, 16 * 12)
                for l in (1, 2, 3):
                    if l > 1:
                        pe.wait_ge(w_turn_kept, l - 1)
                    pe.transpose(ps[:, 2, 0:P], Wl[l][:, :], ident[:, :]).then_inc(w_turned, 1)
                    pe.wait_ge(w_turn_kept, l)
                    pe.wait_ge(avec_made, 2 * l)
                    if l > 1:
                        pe.wait_ge(arows_kept, l - 1)
                    for h in range(2):
                        pe.matmul(ps[:, 1, h * D:(h + 1) * D], avec[:, h, :], WT[:, :], start=True, stop=True)\
                            .then_inc(arows_summed, 1)
                pe.wait_ge(fills_made, 3)
                pe.matmul(ps[:, 0, 0:2], bcols[:, :], acol[2][:, :], start=True, stop=True).then_inc(bias_scored, 1)
                pe.wait_ge(arows_kept, 3)

            def spread_w(l, s):
                n = w_count(l, s)
                pe.wait_ge(diag_made, n + 1)
                if not (isinstance(n, int) and n == 0):
                    pe.wait_ge(w_kept, n)
                pe.matmul(ps[:, w_bank(l, s), :], ones[:, :], w_diag[:, :, :].rearrange("p t i -> p (t i)"),
                          start=True, stop=True).then_inc(w_spread, 1)

            def between(l):
                if l == 0:
                    spread_w(0, 0)
                    for t in range(TILES - 1):
                        turn_piece(0, 0, t)
                    pe.wait_ge(w_kept, 1)
                    make_constants()
                    turn_piece(0, 0, TILES - 1)
                pe.wait_ge(x_added, (l + 1) * S)
                for t in range(TILES):
                    last = pe.matmul(X_SUM, xsums[:, t, :], ones[:, 0:1], start=t == 0, stop=t == TILES - 1)
                last.then_inc(x_summed, 1)
                pe.wait_ge(xrows_made, l + 1)
                of_mean = pe.matmul(ps[:, MEAN_BANK, 0:D], xrows[:, :], Wl[l][:, :] if l else ident[:, :],
                                    start=True, stop=l not in bias_rows)
                if l in bias_rows:
                    of_mean = pe.matmul(ps[:, MEAN_BANK, 0:D], ident[:, :], bias_rows[l][:, :],
                                        start=False, stop=True)
                of_mean.then_inc(mean_summed, 1)
                if l > 1:
                    spread_w(l, 0)
                if l == 0:
                    pe.wait_ge(y0_made, 2)
                pe.wait_ge(mean_kept, l + 1)

            def superblock0(s, slot, first, last):
                if not (isinstance(s, int) and s < 2):
                    pe.wait_ge(scored, S + s - 1)
                for k in range(2):
                    pe.matmul(sums0(slot)[:, 2 * k:2 * k + 2, 0:VC], zeros[:, 0:P], zeros[:, 0:2 * VC],
                              start=True, stop=False, skip_group_check=True)
                for m in range(PARTS):
                    end = m == PARTS - 1
                    if first and m:
                        pe.wait_ge(y0_more, m)
                    for c in range(CHUNKS):
                        pe.wait_ge(pair_made, s * NC + CHUNKS * m + c + 1)
                        for b in range(2):
                            for t in range(TILES):
                                mm = pe.matmul(sums0(slot)[:, t, 0:VC], pair[:, c % RING, b, t * P:(t + 1) * P],
                                               y[:, PB * m + 2 * c + b, :], start=False,
                                               stop=end and c == CHUNKS - 1 and b == 1, skip_group_check=True)
                        mm.then_inc(pair_free, 1)
                        if m == 3 and c == 0 and not last:
                            pe.wait_ge(w_kept, s + 2)
                        if c < TILES and (not end or not last):
                            turn_piece(s if not end else s + 1, (m + 1) % PARTS, c)
                        if m == 2 and c == CHUNKS - 1 and not last:
                            pe.wait_ge(piece_kept, TILES * (s * PARTS + 3) + 1)
                            spread_w(0, s + 1)

            def natural_sums(l, s):
                pe.wait_ge(aggr_kept, (l - 1) * S + s + 1)
                if not (isinstance(s, int) and s == 0 and l == 1):
                    pe.wait_ge(sums_read, l * S + s)
                for t in range(TILES):
                    last = pe.matmul(NAT[:, t, 0:VC], aggr[:, t * P:(t + 1) * P], Wnat[l][:, :],
                                     start=t % 2 == 0, stop=True, skip_group_check=True)
                last.then_inc(rows_summed, 1)

            def superblock(l, s, first, last):
                to = sumsT(s % 2)
                for c in range(NC):
                    if l > 1 and first and c == 0:
                        pe.wait_ge(y_full_made, l - 1)
                    if l == 1 and first and c % 2 == 0:
                        pe.wait_ge(y_made, y_count(l, c // 2 + 1))
                    opens, ends = c == 0, c == NC - 1
                    if l == 1:
                        pe.wait_ge(pair_made, (S + s) * NC + c + 1)
                        for b in range(2):
                            for part in range(2):
                                mm = pe.matmul(to, y1_r[:, 2 * c + b, part, :], bits_r[:, c % RING, b, :],
                                               start=opens and b + part == 0, stop=ends and b + part == 2,
                                               skip_group_check=True)
                        mm.then_inc(pair_free, 1)
                    else:
                        pe.wait_ge(full_made, split_count(l, s, c + 1))
                        pe.matmul(to, y_full[:, c, :], full[:, c % RING, :], start=opens, stop=False,
                                  skip_group_check=True).then_inc(full_free, 1)
                        if first and c % 2 == 0:
                            pe.wait_ge(y_made, y_count(l, c // 2 + 1))
                        high, low = split_hi[:, c % RING, :], split_lo[:, c % RING, :]
                        pe.wait_ge(high_made, split_count(l, s, c + 1))
                        pe.matmul(to, y_split_r[:, c, 0, :], high, start=False, stop=False, skip_group_check=True)
                        pe.matmul(to, y_split_r[:, c, 1, :], high, start=False, stop=False, skip_group_check=True)
                        pe.wait_ge(low_made, RING + split_count(l, s, c + 1))
                        pe.matmul(to, y_split_r[:, c, 0, :], low, start=False, stop=ends,
                                  skip_group_check=True).then_inc(split_free, 1)
                    if l > 1 and c == 6 and not last:
                        spread_w(l, s + 1)
                    if first:
                        continue
                    if c == 1:
                        natural_sums(l, s - 1)

            pe.sem_inc(full_free, RING)
            pe.sem_inc(split_free, RING)
            between(0)
            superblock0(0, 0, True, False)
            with pe.Fori(1, S - 2, 2) as s:
                superblock0(s, 1, False, False)
                superblock0(s + 1, 0, False, False)
            superblock0(S - 1, 1, False, True)
            for l in range(1, LAYERS):
                between(l)
                superblock(l, 0, True, False)
                with pe.Fori(1, S - 1) as s:
                    superblock(l, s, False, False)
                superblock(l, S - 1, False, True)
                natural_sums(l, S - 1)

        @block.vector
        def _(dve):
            chain = Chain(dve, vec_step)
            nc.vector.memset(ones[:, :], 1.0).then_inc(fills_made, 1)
            nc.vector.memset(zeros[:, :], 0.0).then_inc(fills_made, 1)

            def compare_piece(s, m, t):
                g = s * PARTS + m
                dve.wait_ge(adj_loaded[t], 16 * (g + 1))
                if not (isinstance(g, int) and g == 0):
                    dve.wait_ge(piece_turned, (g - 1) * TILES + t + 1)
                nc.vector.tensor_scalar(bytes_in[:, t, :], adj_in[:, t, :], 0.0, None, ALU.is_gt)\
                    .then_inc(piece_compared, 1)

            def score_rows(l, s, t, rows, which=None):
                if t == 0 and not (isinstance(s, int) and s == 0 and l == 0):
                    dve.wait_ge(scored, l * S + s)
                for h in which or ((0, 1) if l in HAS_S else (1,)):
                    last = nc.vector.scalar_tensor_tensor(
                        (G, Z)[h][:, t, :], rows, 1.0, arows[l][:, h, :], ALU.mult, ALU.mult,
                        accum_out=scores[:, bass.ds(TILES * s + t, 1), h])
                if t == TILES - 1:
                    last.then_inc(scored, 1)

            dve.wait_ge(scores_loaded, 16)
            for s in range(S):
                dve.wait_ge(x_loaded[4 * s // S], 16)
                for t in range(TILES):
                    score_rows(0, s, t, X[:, TILES * s + t, :], (1,))

            def score_s(s, t):
                n = nc.vector.scalar_tensor_tensor(
                    G[:, t, :], X[:, bass.ds(TILES * s + t, 1), :].rearrange("p a d -> p (a d)"), 1.0,
                    arows[0][:, 0, :], ALU.mult, ALU.mult, accum_out=scores[:, bass.ds(TILES * s + t, 1), 0])
                if t == TILES - 1:
                    n.then_inc(s_scored, 1)
                    dve.wait_ge(s_scored, s + 1)
                    nc.vector.tensor_scalar(wcol[:, bass.ds(TILES * s, TILES)], scores[:, bass.ds(TILES * s, TILES), 0],
                                            tmax[:, 0:1], CAP / (1.0 - SLOPE[0]), ALU.add, ALU.min)\
                        .then_inc(w_asked, 1)

            def make_constants():
                dve.wait_ge(consts_loaded, 16 * 12)
                dve.wait_ge(fills_made, 2)
                nc.vector.tensor_scalar(bcols[:, :], ones[:, :], bcol[:, 0:1], None, ALU.mult).then_inc(fills_made, 1)
                nc.vector.memset(beta[:, :], 0.0).then_inc(fills_made, 1)
                for l in (1, 2, 3):
                    dve.wait_ge(w_turned, l)
                    if l > 1:
                        dve.wait_ge(arows_summed, 2 * (l - 1))
                    nc.vector.tensor_copy(WT[:, :], ps[:, 2, 0:P]).then_inc(w_turn_kept, 1)
                    for h in range(2):
                        nc.vector.tensor_scalar(avec[:, h, :], ones[:, :], acol[l][:, h:h + 1], None, ALU.mult)\
                            .then_inc(avec_made, 1)
                    dve.wait_ge(arows_summed, 2 * l)
                    nc.vector.tensor_copy(arows[l][:, :, :].rearrange("p h k -> p (h k)"), ps[:, 1, 0:2 * D])\
                        .then_inc(arows_kept, 1)
                dve.wait_ge(bias_scored, 1)
                dve.wait_ge(fills_made, 4)
                chain.then(nc.vector.tensor_copy(bdot[:, :], ps[:, 0, 0:2]))
                dve.wait_ge(ident_made, 2)
                for l in (1, 2, 3):
                    chain.then(nc.vector.tensor_tensor(Wnat[l][:, 0:D], Wl[l][:, :], Wnat[l][:, 0:D], ALU.subtract))
                    nc.vector.tensor_copy(Wnat[l][:, D:VC], ident[:, DL:D]).then_inc(wnat_made, 1)
                for l in bias_rows:
                    nc.vector.scalar_tensor_tensor(Wnat[l][:, 0:D], bias_rows[l][:, :], ident[:, DL:D],
                                                   Wnat[l][:, 0:D], ALU.mult, ALU.add).then_inc(wnat_made, 1)
                dve.wait_ge(wnat_made, 5)
                chain.then(nc.vector.tensor_tensor(beta[:, :], bdot[:, 0:1], bdot[:, 1:2], ALU.add))

            def between(l):
                dve.wait_ge(scored, (l + 1) * S)
                nc.vector.tensor_reduce(tpart[:, :], scores[:, :, 1], AX.X, ALU.max).then_inc(tpart_made, 1)
                dve.wait_ge(tmax_made, l + 1)
                chain.then(nc.vector.tensor_scalar(tcol[:, :], scores[:, :, 1], tmax[:, 0:1], None, ALU.subtract))
                if l != 1:
                    chain.then(nc.vector.tensor_scalar(ccol[:, :], tcol[:, :], -(1.0 - SLOPE[l]), CAP,
                                                       ALU.mult, ALU.min))
                    if l == 2:
                        chain.then(nc.vector.tensor_tensor(sbias[:, :], tmax[:, :], beta[:, :], ALU.add))
                    if l:
                        guard = sbias if l == 2 else tmax
                        chain.then(nc.vector.tensor_scalar(wcol[:, :], scores[:, :, 0], guard[:, 0:1],
                                                           CAP / (1.0 - SLOPE[l]), ALU.add, ALU.min))
                nc.vector.tensor_scalar(vcol[:, :], tcol[:, :], KAPPA, None, ALU.subtract)\
                    .then_inc(exponents_made, 1)
                if l == 0:
                    for t in range(TILES):
                        score_s(0, t)
                    dve.wait_ge(exps_made, 1)
                    nc.vector.tensor_tensor(y[:, 0:PB, 0:D], X[:, 0:PB, :],
                                            vcol[:, 0:PB].rearrange("p (q a) -> p q a", a=1).broadcast_to([P, PB, D]),
                                            ALU.mult).then_inc(y0_made, 1)
                    for t in range(TILES - 1):
                        compare_piece(0, 0, t)
                    make_constants()
                dve.wait_ge(x_summed, l + 1)
                chain.then(nc.vector.tensor_copy(xtot[:, :], X_SUM))
                if l:
                    dve.wait_ge(mean_summed, l)
                nc.vector.tensor_scalar(xrows[:, :], ones[:, :], xtot[:, 0:1], 1.0 / N, ALU.mult, ALU.mult)\
                    .then_inc(xrows_made, 1)
                dve.wait_ge(exps_made, l + 1)
                if l > 1:
                    v = vcol[:, :].rearrange("p (c b) -> p c b", b=2)
                    nc.vector.tensor_copy(y_full[:, :, DL], v[:, :, 0])
                    nc.vector.tensor_tensor(y_full[:, :, 0:DL],
                                            X[:, :, :].rearrange("p (c b) d -> p c b d", b=2)[:, :, 0, 0:DL],
                                            v[:, :, 0:1].broadcast_to([P, NC, DL]), ALU.mult)\
                        .then_inc(y_full_made, 1)

            def step(l, s, slot, m, c, ring):
                if l < 2:
                    dve.wait_ge(pair_free, (l * S + s) * NC + CHUNKS * m + c + 1)
                for b in range(2):
                    if l < 2:
                        to, made = (pair, bits_r)[l][:, ring, b, :], pair_made
                    elif b == 0:
                        dve.wait_ge(full_free, split_count(l, s, CHUNKS * m) + c + 1)
                        to, made = full[:, ring, :], full_made
                    else:
                        dve.wait_ge(low_made, split_count(l, s, CHUNKS * m) + c + 1)
                        to, made = split[:, ring, :], split_made
                    bits = pairs[:, m, :, bass.ds(c, 1), :, b].rearrange("p t c i -> p t (c i)")
                    weights = to.rearrange("p (t i) -> p t i", t=TILES)
                    if l == 1:
                        done = nc.vector.tensor_copy(weights, bits)
                    else:
                        done = nc.vector.scalar_tensor_tensor(
                            weights, w_rows[:, slot, :].rearrange("p (t i) -> p t i", t=TILES),
                            ccol[:, bass.ds(PB * m + c * 2 + b, 1)], bits, ALU.max, ALU.mult)
                    if b or l > 1:
                        done.then_inc(made, 1)

            def tail(l, s, slot, base):
                chain.at = base
                old = X[:, bass.ds(TILES * s, TILES), :]
                got = natural(l, slot)
                if l == 0:
                    dve.wait_ge(pair_free, RING + (s + 1) * NC)
                else:
                    dve.wait_ge(rows_summed, (l - 1) * S + s + 1)
                chain.then(nc.vector.tensor_scalar(flag[:, :], got[:, :, D], 0.0, None, ALU.is_equal))
                chain.then(nc.vector.tensor_tensor(den[:, :], got[:, :, D], flag[:, :], ALU.add))
                chain.then(nc.vector.reciprocal(rinv[:, :], den[:, :]))
                yield
                dve.wait_ge(mean_kept, l + 1)
                dve.wait_ge(scored, (l + 1) * S + (s if l < LAYERS - 1 else 0))
                if l == LAYERS - 1:
                    dve.wait_ge(x_new, l * S + s)
                for t in range(TILES):
                    if l < LAYERS - 1:
                        g = nc.vector.scalar_tensor_tensor(G[:, t, :], mean[:, :], flag[:, t:t + 1],
                                                           X[:, bass.ds(TILES * s + t, 1), :].rearrange("p a d -> p (a d)"),
                                                           ALU.mult, ALU.add)
                    else:
                        g = nc.vector.tensor_scalar(G[:, t, :], mean[:, :], flag[:, t:t + 1], None, ALU.mult)
                chain.then(g)
                yield
                for t in range(TILES):
                    z = nc.vector.scalar_tensor_tensor(Z[:, t, :], got[:, t, 0:D], rinv[:, t:t + 1], G[:, t, :],
                                                       ALU.mult, ALU.add)
                z.then_inc(sums_read, 1)
                dve.wait_ge(sums_read, l * S + s + 1)
                yield
                if l == LAYERS - 1:
                    nc.vector.tensor_scalar(G[:, :, :], Z[:, :, :], 0.0, None, ALU.min).then_inc(elu_asked, 1)
                    chain.then(nc.vector.tensor_scalar(Z[:, :, :], Z[:, :, :], 0.0, None, ALU.max))
                    yield
                    dve.wait_ge(elu_done, s + 1)
                    chain.then(nc.vector.scalar_tensor_tensor(Z[:, :, :], G[:, :, :], -1.0, Z[:, :, :],
                                                              ALU.add, ALU.add))
                    yield
                    chain.then(nc.vector.tensor_tensor(Z[:, :, :], Z[:, :, :], old, ALU.add))
                    yield
                for t in range(TILES):
                    b = nc.vector.bn_stats(stats[:, t, :], Z[:, t, :])
                chain.then(b)
                yield
                dve.sem_inc(dve_waited, 1)
                for t in range(TILES):
                    b = nc.vector.bn_aggr(mv[:, t, :], stats[:, t, :])
                chain.then(b)
                nc.vector.tensor_scalar(spread[:, :], mv[:, :, 1], EPS, None, ALU.add).then_inc(moments_made, 1)
                nc.vector.tensor_scalar(minus[:, :], mv[:, :, 0], -1.0, None, ALU.mult).then_inc(moments_made, 1)

            def superblock(l, s, slot, first, last, base):
                for m in range(PARTS):
                    loaded = (piece_kept, TILES * (s * PARTS + m + 1)) if l == 0 else \
                        (mask_loaded[m], 16 * ((l - 1) * S + s + 1))
                    behind = not first and m == 1
                    if l != 1 and m == 0:
                        dve.wait_ge(w_kept, w_count(l, s) + 1)
                    if behind:
                        stages = tail(l, s - 1, 1 - slot, base + (s - 1) * TAIL[l])
                    dve.wait_ge(*loaded)
                    for c in range(CHUNKS):
                        if l == 0 and c < TILES - 1 and (m + 1 < PARTS or not last):
                            compare_piece(s if m + 1 < PARTS else s + 1, (m + 1) % PARTS, c)
                        step(l, s, slot, m, c, c % RING)
                        if l == 0 and m == 0 and c < TILES and not last:
                            score_s(s + 1, c)
                        if behind:
                            next(stages, None)
                        if m == PARTS - 1 and not first and l < LAYERS - 1 and 1 <= c <= TILES:
                            dve.wait_ge(x_new, l * S + s)
                            score_rows(l + 1, s - 1, c - 1, Xnew[:, c - 1, :])
                    if behind:
                        assert next(stages, 0) == 0

            for l in range(LAYERS):
                between(l)
                base = chain.at
                superblock(l, 0, 0, True, False, base)
                with dve.Fori(1, S - 2, 2) as s:
                    superblock(l, s, 1, False, False, base)
                    superblock(l, s + 1, 0, False, False, base)
                superblock(l, S - 1, 1, False, True, base)
                for _ in tail(l, S - 1, 1, base + (S - 1) * TAIL[l]):
                    pass
                if l < LAYERS - 1:
                    dve.wait_ge(x_new, (l + 1) * S)
                    for t in range(TILES):
                        score_rows(l + 1, S - 1, t, Xnew[:, t, :])


_INS = ["x", "adj", "L0_gnn_a", "L1_gnn_W_fc", "L1_gnn_b_fc", "L1_gnn_w_att", "L2_gnn_W_w", "L2_gnn_W_b",
        "L2_gnn_a", "L3_gnn_W", "L3_gnn_a"]


def kernel(**inputs):
    import numpy as _np
    import concourse.bacc as _bacc
    from concourse import mybir as _mybir
    from concourse.bass_utils import run_bass_kernel_spmd as _run

    nc = _bacc.Bacc("TRN2", target_bir_lowering=False, num_devices=1)
    arrays, args = {}, []
    for name in _INS:
        a = _np.ascontiguousarray(inputs[name])
        if name.endswith("_a"):
            a = a.reshape(-1)
        arrays[f"in_{name}_dram"] = a
        args.append(nc.dram_tensor(f"in_{name}_dram", a.shape, _mybir.dt.from_np(a.dtype), kind="ExternalInput").ap())
    n, d = inputs["x"].shape
    args.append(nc.dram_tensor("out_0_dram", (n, d), _mybir.dt.float32, kind="ExternalOutput").ap())
    gat4(nc, *args)
    r = _run(nc, [arrays], core_ids=[0])
    return r.results[0]["out_0_dram"]
```
